# Optimizing a Trainium2 kernel written in Bass

```python
import numpy as np
import jax
import jax.numpy as jnp

def _softmax(x, axis=-1):
    return jax.nn.softmax(x, axis=axis)

def _gelu(x):
    return jax.nn.gelu(x, approximate=True)

def _silu(x):
    return jax.nn.silu(x)

def _sigmoid(x):
    return jax.nn.sigmoid(x)

def _layernorm(x, axis=-1, eps=1e-05):
    m = jnp.mean(x, axis=axis, keepdims=True)
    v = jnp.var(x, axis=axis, keepdims=True)
    return (x - m) / jnp.sqrt(v + eps)

def _scatter_add(tgt, idx, src, axis=0):
    return tgt.at[idx].add(src)

def _segment_sum(src, seg, n):
    return jax.ops.segment_sum(src, seg, n)
kernel_name = 'mk_xattn_ffn_d1_seqx_r8_0d9b15'

def setup_inputs(seed: int=0):
    np.random.seed(seed)
    _w = jnp.asarray

    def _rec_inputs():
        import jax
        import jax.numpy as jnp
        _rk = jax.random.key(seed)
        x = -0.0002928 + 1 * jax.random.normal(jax.random.fold_in(_rk, 1), (32, 128, 128), jnp.float32)
        _lenS = 128 - jax.random.randint(jax.random.fold_in(_rk, 7), (32,), 0, max(1, 128 // 4) + 1, jnp.int32)
        _lenS2 = 128 - jax.random.randint(jax.random.fold_in(_rk, 8), (32,), 0, max(1, 128 // 4) + 1, jnp.int32)
        _ctx_1024P = jax.random.normal(jax.random.fold_in(_rk, 11), (32, 16, 128), jnp.float32)
        _ctx_1024c = jax.random.dirichlet(jax.random.fold_in(_rk, 511), 0.3 * jnp.ones((16,), jnp.float32), (32, 128))
        _ctx_1024t = jnp.einsum('bsk,bkd->bsd', _ctx_1024c, _ctx_1024P)
        _ctx_1024t = _ctx_1024t * jax.lax.rsqrt(jnp.mean(jnp.square(_ctx_1024t)) + 1e-12) * 0.953939
        ctx_1024 = -1.39393e-06 + 0.999914 * (_ctx_1024t + 0.3 * jax.random.normal(jax.random.fold_in(_rk, 611), (32, 128, 128), jnp.float32))
        return (x, ctx_1024)
    x, ctx_1024 = _rec_inputs()

    def _L0_xattn_setup():
        import jax, jax.numpy as jnp
        import numpy as np
        E = 128
        H = 16
        D = E // H
        B, S = (2, 256)

        def _xavier(key, shape):
            fan_in, fan_out = (shape[1], shape[0])
            limit = float(np.sqrt(6.0 / (fan_in + fan_out)))
            return jax.random.uniform(key, shape, jnp.float32, -limit, limit)
        key = jax.random.key(seed)
        ks = jax.random.split(key, 7)
        return {'query': jax.random.normal(ks[0], (B, S, E), jnp.float32), 'key': jax.random.normal(ks[1], (B, S, E), jnp.float32), 'value': jax.random.normal(ks[2], (B, S, E), jnp.float32), 'Wq': _xavier(ks[3], (E, E)), 'bq': jnp.zeros((E,), jnp.float32), 'Wk': _xavier(ks[4], (E, E)), 'bk': jnp.zeros((E,), jnp.float32), 'Wv': _xavier(ks[5], (E, E)), 'bv': jnp.zeros((E,), jnp.float32), 'Wo': _xavier(ks[6], (E, E)), 'bo': jnp.zeros((E,), jnp.float32)}
    _L0_xattn_all = _L0_xattn_setup()
    _L0_xattn_in = {k: v for k, v in _L0_xattn_all.items() if k in ('Wq', 'bq', 'Wk', 'bk', 'Wv', 'bv', 'Wo', 'bo')}
    del _L0_xattn_all

    def _L0_ffn_setup():
        import jax, jax.numpy as jnp
        import numpy as np
        B, S, D, E = (4, 256, 128, 8)
        key = jax.random.key(seed)
        ks = jax.random.split(key, 5)
        s = 0.02
        return {'hidden_states': jax.random.normal(ks[0], (B, S, D), dtype=jnp.float32), 'Wr': jax.random.normal(ks[1], (D, E), dtype=jnp.float32) * s, 'br': jnp.zeros((E,), dtype=jnp.float32), 'W1': jax.random.normal(ks[2], (E, D, 4 * D), dtype=jnp.float32) * s, 'b1': jnp.zeros((E, 4 * D), dtype=jnp.float32), 'W2': jax.random.normal(ks[3], (E, 4 * D, 2 * D), dtype=jnp.float32) * s, 'b2': jnp.zeros((E, 2 * D), dtype=jnp.float32), 'W3': jax.random.normal(ks[4], (E, 2 * D, D), dtype=jnp.float32) * s, 'b3': jnp.zeros((E, D), dtype=jnp.float32)}
    _L0_ffn_all = _L0_ffn_setup()
    _L0_ffn_in = {k: v for k, v in _L0_ffn_all.items() if k in ('Wr', 'br', 'W1', 'b1', 'W2', 'b2', 'W3', 'b3')}
    del _L0_ffn_all
    return {'x': x, 'ctx_1024': ctx_1024, 'L0_xattn_Wq': _L0_xattn_in['Wq'], 'L0_xattn_bq': _L0_xattn_in['bq'], 'L0_xattn_Wk': _L0_xattn_in['Wk'], 'L0_xattn_bk': _L0_xattn_in['bk'], 'L0_xattn_Wv': _L0_xattn_in['Wv'], 'L0_xattn_bv': _L0_xattn_in['bv'], 'L0_xattn_Wo': _L0_xattn_in['Wo'], 'L0_xattn_bo': _L0_xattn_in['bo'], 'L0_ffn_Wr': _L0_ffn_in['Wr'], 'L0_ffn_br': _L0_ffn_in['br'], 'L0_ffn_W1': _L0_ffn_in['W1'], 'L0_ffn_b1': _L0_ffn_in['b1'], 'L0_ffn_W2': _L0_ffn_in['W2'], 'L0_ffn_b2': _L0_ffn_in['b2'], 'L0_ffn_W3': _L0_ffn_in['W3'], 'L0_ffn_b3': _L0_ffn_in['b3']}

def reference(x, ctx_1024, L0_xattn_Wq, L0_xattn_bq, L0_xattn_Wk, L0_xattn_bk, L0_xattn_Wv, L0_xattn_bv, L0_xattn_Wo, L0_xattn_bo, L0_ffn_Wr, L0_ffn_br, L0_ffn_W1, L0_ffn_b1, L0_ffn_W2, L0_ffn_b2, L0_ffn_W3, L0_ffn_b3):
    import jax
    import jax.numpy as jnp

    def _L0_xattn_ref(query, key, value, Wq, bq, Wk, bk, Wv, bv, Wo, bo):
        import jax, jax.numpy as jnp
        import numpy as np
        E = 128
        H = 16
        D = E // H
        B, S = (2, 256)

        def _xavier(key, shape):
            fan_in, fan_out = (shape[1], shape[0])
            limit = float(np.sqrt(6.0 / (fan_in + fan_out)))
            return jax.random.uniform(key, shape, jnp.float32, -limit, limit)
        b, s, e = query.shape
        Q = (query @ Wq.T + bq).reshape(b, s, H, D).transpose(0, 2, 1, 3)
        K = (key @ Wk.T + bk).reshape(b, s, H, D).transpose(0, 2, 1, 3)
        V = (value @ Wv.T + bv).reshape(b, s, H, D).transpose(0, 2, 1, 3)
        scale = D ** (-0.5)
        scores = jnp.einsum('bhqd,bhkd->bhqk', Q, K) * scale
        attn = jax.nn.softmax(scores, axis=-1)
        out = jnp.einsum('bhqk,bhkd->bhqd', attn, V)
        out = out.transpose(0, 2, 1, 3).reshape(b, s, e)
        return out @ Wo.T + bo

    def _L0_ffn_ref(hidden_states, Wr, br, W1, b1, W2, b2, W3, b3):
        import jax, jax.numpy as jnp
        import numpy as np
        B, S, D, E = (4, 256, 128, 8)
        b, s, d = hidden_states.shape
        num_experts = Wr.shape[1]
        x = hidden_states.reshape(-1, d)
        router_logits = x @ Wr + br
        expert_mask = jax.nn.one_hot(jnp.argmax(router_logits, axis=-1), num_experts, dtype=x.dtype)
        out = jnp.zeros_like(x)
        for e in range(num_experts):
            h = jax.nn.gelu(x @ W1[e] + b1[e], approximate=False)
            h = jax.nn.gelu(h @ W2[e] + b2[e], approximate=False)
            y = h @ W3[e] + b3[e]
            out = out + expert_mask[:, e:e + 1] * y
        return out.reshape(b, s, d)
    x = x + _L0_xattn_ref(_layernorm(x, axis=-1), ctx_1024, ctx_1024, L0_xattn_Wq, L0_xattn_bq, L0_xattn_Wk, L0_xattn_bk, L0_xattn_Wv, L0_xattn_bv, L0_xattn_Wo, L0_xattn_bo)
    x = x + _L0_ffn_ref(_layernorm(x, axis=-1), L0_ffn_Wr, L0_ffn_br, L0_ffn_W1, L0_ffn_b1, L0_ffn_W2, L0_ffn_b2, L0_ffn_W3, L0_ffn_b3)
    return x

_drawn_inputs = setup_inputs


def setup_inputs(seed=0):
    import zlib

    import numpy as np

    out = dict(_drawn_inputs(seed))
    spreads = {'L0_xattn_bq': (0.0, 0.298),
     'L0_xattn_bk': (0.0, 0.8),
     'L0_xattn_bv': (0.0, 0.1),
     'L0_xattn_bo': (0.0, 0.1),
     'L0_ffn_br': (0.0, 0.1),
     'L0_ffn_b1': (0.0, 0.8),
     'L0_ffn_b2': (0.0, 0.56),
     'L0_ffn_b3': (0.0, 0.1)}
    factors = {'L0_ffn_W1': 7.506, 'L0_ffn_W2': 6.878, 'L0_ffn_W3': 3.353}
    for name, (base, spread) in spreads.items():
        noise = np.random.default_rng([zlib.crc32(name.encode()), seed]).standard_normal(out[name].shape)
        drawn = base * np.exp(spread * noise) if base else spread * noise
        out[name] = jnp.asarray(drawn.astype(out[name].dtype))
    for name, factor in factors.items():
        out[name] = (out[name] * factor).astype(out[name].dtype)
    return out
```

```python
import concourse.bass as bass
from concourse import mybir
from contextlib import ExitStack

F32 = mybir.dt.float32
F32R = mybir.dt.float32r
BF16 = mybir.dt.bfloat16
I32 = mybir.dt.int32
ALU = mybir.AluOpType
ACT = mybir.ActivationFunctionType
AX = mybir.AxisListType

P = 128
D = 128
NB = 32
NH = 16
DH = 8
NG = 4
NJ = 4
PAIRS = NB // 2
T = 2 * P
NE = 8
D1, D2 = 4 * D, 2 * D
EPS = 1e-5
SCALE = DH ** -0.5
TOKENS = NB * P
REGION = TOKENS + P
ROW = 2 * D + 1
NT = NB + NE - 1
WB = NE * REGION
NU = 3
NG6 = 2 * NU
WA = D1 + 2 * D + 6

C_ID, C_LT, C_ONE, C_MASK, C_FIRST, C_REGION, C_TRI, C_JT = 0, P, 2 * P, 3 * P, 3 * P + 4, 3 * P + 12, 3 * P + 20, 3 * P + 84
C_HALF = C_JT + NT
C_TOK = C_HALF + 2
C_ALL = C_TOK + NB


def build(nc, x, ctxT, wqT, wkT, wvT, woT, bqk, bv, bo, wr, br, wa, w2, b3, cst, tok, out):
    scratch = nc.dram_tensor("scratch", (WB + P, ROW), F32, kind="Internal").ap()
    ctx = ExitStack()
    with ctx:
        def sb(name, shape, dt=F32, where=ctx):
            return where.enter_context(nc.sbuf_tensor(name, shape, dt))

        def sem(name):
            return ctx.enter_context(nc.semaphore(name))

        C = sb("C", [P, C_ALL])
        Tok = sb("Tok", [P, NB], I32)
        LtOne = sb("LtOne", [P, 2, P], BF16)
        WqkT = sb("WqkT", [P, 2, D])
        WvT = sb("WvT", [P, D])
        WoT = sb("WoT", [P, D])
        Bqk = sb("Bqk", [P, 2])
        Bv = sb("Bv", [P, D])
        Bo = sb("Bo", [P, D])
        Wr = sb("Wr", [P, NE])
        Br = sb("Br", [P, NE])
        WAll = sb("WAll", [P, NE, WA])
        W2All = sb("W2All", [P, NE, 4 * D2])
        B3 = sb("B3", [P, NE, D])
        X = sb("X", [P, NB, D])
        ident = C[:, C_ID:C_ID + P]
        stats = sb("stats", [P, 2, 6])
        mv = sb("mv", [P, 2, 2])
        rstd = sb("rstd", [P, 2])
        xn = sb("xn", [P, 2, D])
        stats2 = sb("stats2", [P, 6])
        mv2 = sb("mv2", [P, 2, 2])
        rstd2 = sb("rstd2", [P, 2])
        nrm2 = sb("nrm2", [P, 2])
        negmax = sb("negmax", [P, NH])
        shift = sb("shift", [P, 2 * NH])
        rec = sb("rec", [P, NH])
        logit = sb("logit", [P, 2, NE])
        pick = sb("pick", [P, 2, NE])
        best = sb("best", [P, 2])
        onehot = sb("onehot", [P, 2, NE], BF16)
        rank = sb("rank", [P, 2, NE])
        posf = sb("posf", [P, 2])
        pos = sb("pos", [P, 2, 2], I32)
        base = sb("base", [P, NE])
        Row = sb("Row", [P, 2, 2, ROW])
        padrow = sb("padrow", [P, NE], I32)
        PadTile = sb("PadTile", [P, ROW])
        with ExitStack() as att:
            ctxs = sb("ctxs", [P, 2, T], where=att)
            xnT = sb("xnT", [P, T], where=att)
            HL = sb("HL", [P, 4, T], where=att)
            HLm = sb("HLm", [P, 3, NJ, T], where=att)
            Qst = sb("Qst", [P, 2, NG, T], where=att)
            Kbd = sb("Kbd", [P, 2, NG, NJ, T], where=att)
            Kst = sb("Kst", [P, 2, NG, T], where=att)
            Qbd = sb("Qbd", [P, 2, NG, NJ, T], where=att)
            Vst = sb("Vst", [P, 2, 2, 8, DH, 4], where=att)
            shiftT = sb("shiftT", [2 * NH, P], where=att)
            Ex = sb("Ex", [P, NG, NJ * P], where=att)
            OTs = sb("OTs", [P, 4 * P], where=att)
            On = sb("On", [P, D], where=att)
            OT = sb("OT", [P, P], where=att)
            x2T = sb("x2T", [P, T], where=att)
        with ExitStack() as ffn:
            cnt = sb("cnt", [P, NE], where=ffn)
            cnti = sb("cnti", [P, NE], I32, where=ffn)
            ntile = sb("ntile", [P, NE], where=ffn)
            cumw = sb("cumw", [P, NE, NE], where=ffn)
            cum = sb("cum", [P, NE], where=ffn)
            past = sb("past", [P, NT, NE], where=ffn)
            pastn = sb("pastn", [P, NT, NE], where=ffn)
            texp = sb("texp", [P, NT], where=ffn)
            tdone = sb("tdone", [P, NT], where=ffn)
            wexp_i = sb("wexp_i", [P, NT], I32, where=ffn)
            trow_i = sb("trow_i", [P, NT], I32, where=ffn)
            G = sb("G", [P, 2 * NU, ROW], where=ffn)
            GT = sb("GT", [P, NU, P], where=ffn)
            Ws = sb("Ws", [P, NU, WA], where=ffn)
            W2s = sb("W2s", [P, NU, 4 * D2], where=ffn)
            H1 = sb("H1", [P, NU, 4, P], where=ffn)
            H2 = sb("H2", [P, NU, 2, P], where=ffn)
            XB = sb("XB", [P, NU, D], where=ffn)
            OUT = sb("OUT", [P, NU, D], where=ffn)

        ps = [ctx.enter_context(nc.psum_tensor(f"bank{k}", [P, 512], F32)) for k in range(8)]
        psT, psS, psO, psD, psA, psM = ps[0:2], ps[2:4], ps[4], ps[5], ps[6], ps[7]
        ps1, ps2, psY, psX = ps[0:4], ps[4:6], ps[6], ps[7]

        S = {}
        for name in """x_in ctx_in wqk_in wv_in wo_in small_in w_in tok_in
                const_zero lt_ready bd_zero
                ln_stats ln_rstd xn_ready xnT_ps xnT_sb v_ps v_sb qk_ps hi_ready lo_ready masked masked_act
                s_in st_in s_ps max_done shT_ps shT_sb shift_in
                st_ps exp_done pv_ps ot_sb d_ps on_ready e_ps oT_sb f_ps res_ready x2_ready x2n_ready
                ln2_stats x2T_ps x2T_sb lg_ps onehot_ready rk_ps pos_ready scattered
                c_ln c_shift c_norm c_res c_ln2 c_lg c_pos c_tab c_pool c_rk
                tables pad_in passed
                g_ps g_sb w_ready l1_ps h1_ready l2_ps h2_ready l3_ps xb_ready y_ready""".split():
            S[name] = sem(name)
        for g in range(NG6):
            S[f"g_in{g}"] = sem(f"g_in{g}")
            S[f"stored{g}"] = sem(f"stored{g}")

        def apart(eng):
            eng.sem_inc(S["passed"], 1)

        TOTAL = {"x_in": 32}
        for names, total in (("xn_ready xnT_ps xnT_sb v_ps v_sb qk_ps lo_ready masked ln_stats ln_rstd", PAIRS),
                             ("ln2_stats x2n_ready x2T_ps x2T_sb lg_ps onehot_ready rk_ps pos_ready", PAIRS),
                             ("hi_ready masked_act", 2 * PAIRS), ("ctx_in", 16 * PAIRS), ("s_in", 32 * PAIRS),
                             ("st_in", 96 * PAIRS), ("shift_in scattered", 16 * NB), ("s_ps st_ps exp_done max_done", 4 * NB),
                             ("c_shift pv_ps", 2 * NB), ("c_pos", 4 * PAIRS),
                             ("shT_ps shT_sb ot_sb d_ps on_ready e_ps oT_sb f_ps res_ready x2_ready", NB)):
            for name in names.split():
                TOTAL[name] = total

        def W(eng, name, value):
            if isinstance(value, int):
                value = min(value, TOTAL.get(name, value))
                if value <= 0:
                    return
            eng.wait_ge(S[name], value)
            if not isinstance(value, int) and eng in (nc.sync, nc.gpsimd):
                apart(eng)

        class Link:

            def __init__(self, eng, name, turn, per):
                self.eng, self.name, self.base, self.per, self.k = eng, name, turn * per, per, 0

            def __call__(self, ins, alone=False):
                self.k += 1
                ins.then_inc(S[self.name], 1)
                value = self.base + self.k
                self.eng.wait_ge(S[self.name], value)
                if alone and not isinstance(value, int):
                    apart(self.eng)

            def end(self):
                assert self.k == self.per, (self.name, self.k)

        FIRST, LAST = -2, PAIRS + 1

        def turns_of(eng, first, stop, by):
            return eng.Fori(first, stop - by + 1, by)

        def all_steps(eng, step):
            for i in range(FIRST, 2):
                step(i, i % 2)
            with turns_of(eng, 2, PAIRS - 2, 2) as i:
                step(i, 0)
                step(i + 1, 1)
            for i in range(PAIRS - 2, LAST + 1):
                step(i, i % 2)

        def on(i, shift, lo=0, hi=PAIRS):
            return not isinstance(i, int) or lo <= i + shift < hi

        def moved(eng, name, m, c):
            eng.wait_ge(S[f"{name}{c % NG6}"], 16 * (m + c // NG6 + 1))
            if not isinstance(m, int) and eng in (nc.sync, nc.gpsimd):
                apart(eng)

        def column(table, m, c):
            return table[0:1, c:c + 1] if isinstance(m, int) else table[0:1, bass.ds(NG6 * m + c, 1)]

        def all_tiles(eng, step, head, tail):
            for c in range(head):
                step(0, c)
            with eng.Fori(0, (NT - head - tail) // NG6) as m:
                for c in range(head, head + NG6):
                    step(m, c)
            for c in range(NT - tail, NT):
                step(0, c)

        block = ctx.enter_context(nc.Block())

        @block.sync
        def _(sp):
            sp.dma_start(X[:, 0:4, :], x[:, 0:4, :]).then_inc(S["x_in"], 16)
            sp.dma_start(C[:], cst).then_inc(S["small_in"], 16)
            sp.dma_start(WqkT[:, 0, :], wqT).then_inc(S["wqk_in"], 16)
            sp.dma_start(WqkT[:, 1, :], wkT).then_inc(S["wqk_in"], 16)
            sp.dma_start(Bqk[:], bqk).then_inc(S["wqk_in"], 16)
            sp.dma_start(WvT[:], wvT).then_inc(S["wv_in"], 16)
            sp.dma_start(Bv[:], bv).then_inc(S["wv_in"], 16)
            sp.dma_start(WoT[:], woT).then_inc(S["wo_in"], 16)
            sp.dma_start(Bo[:], bo).then_inc(S["wo_in"], 16)
            sp.dma_start(Wr[:], wr).then_inc(S["wo_in"], 16)
            sp.dma_start(Br[:], br).then_inc(S["wo_in"], 16)
            sp.dma_start(Tok[:], tok).then_inc(S["tok_in"], 16)
            sp.dma_start(X[:, 4:NB, :], x[:, 4:NB, :]).then_inc(S["x_in"], 16)

            def step(i, par):
                if on(i, 2):
                    W(sp, "qk_ps", i + 1)
                    W(sp, "v_ps", i + 1)
                    sp.dma_start(ctxs[:, par, :], ctxT[:, (i + 2) * T:(i + 3) * T] if isinstance(i, int)
                                 else ctxT[:, bass.ds((i + 2) * T, T)]).then_inc(S["ctx_in"], 16)
                if on(i, 1):
                    W(sp, "masked", i + 2)
                    W(sp, "masked_act", 2 * (i + 2))
                    W(sp, "st_ps", 8 * i)
                    b = (par + 1) % 2
                    for s, part in enumerate((0, 0, 1)):
                        sp.dma_start(Qbd[32 * s:32 * s + 32, b, :, :, :].rearrange("r g j t -> r g (j t)"),
                                     HLm[:, part, :, :].rearrange("p j t -> p (j t)")).then_inc(S["st_in"], 16)
                    for s, part in enumerate((2, 3, 2)):
                        sp.dma_start(Kst[32 * s:32 * s + 32, b, :, :], HL[:, part, :]).then_inc(S["st_in"], 16)
                for k in range(2):
                    n = 2 * i + k
                    if not isinstance(i, int) or 0 <= n + 1 < NB:
                        b = (par + (1 if k else 0)) % 2
                        W(sp, "shT_sb", n + 2)
                        kk = 1 - k
                        W(sp, "st_ps", 4 * (n - 2))
                        sp.dma_start(Qbd[96:98, b, :, :, kk * P:(kk + 1) * P].rearrange("r g j t -> r (g j) t"),
                                     shiftT[:, :]).then_inc(S["shift_in"], 16)
                if on(i, 2):
                    W(sp, "masked", i + 3)
                    W(sp, "masked_act", 2 * (i + 3))
                    W(sp, "s_ps", 8 * (i + 1))
                    if isinstance(i, int) and i == FIRST:
                        sp.wait_ge(S["bd_zero"], 5)
                    sp.dma_start(Qst[0:32, par, :, :], HL[:, 0, :]).then_inc(S["s_in"], 16)
                    sp.dma_start(Kbd[0:32, par, :, :, :].rearrange("r g j t -> r g (j t)"),
                                 HLm[:, 2, :, :].rearrange("p j t -> p (j t)")).then_inc(S["s_in"], 16)
                if not isinstance(i, int):
                    return
                if i == FIRST:
                    sp.dma_start(WAll[:], wa).then_inc(S["w_in"], 16)
                    sp.dma_start(B3[:], b3).then_inc(S["w_in"], 16)
                if i == FIRST + 1:
                    sp.dma_start(W2All[:], w2).then_inc(S["w_in"], 16)

            all_steps(sp, step)

            sp.wait_ge(S["const_zero"], 2)
            sp.dma_start(scratch[WB:WB + P, :], PadTile[:]).then_inc(S["pad_in"], 16)
            sp.wait_ge(S["tables"], 1)
            for e in range(NE):
                r = sp.value_load(padrow[0:1, e:e + 1], min_val=0, max_val=WB - P)
                sp.dma_start(scratch[bass.ds(r, P), :], PadTile[:]).then_inc(S["pad_in"], 16)
            sp.wait_ge(S["scattered"], 16 * NB)
            sp.wait_ge(S["pad_in"], 16 * (NE + 1))
            sp.wait_ge(S["tables"], 3)

            def tile(m, c):
                if c >= NG6:
                    moved(sp, "stored", m, c - NG6)
                r = sp.value_load(column(trow_i, m, c), min_val=0, max_val=WB)
                sp.dma_start(G[:, c % NG6, :], scratch[bass.ds(r, P), :]).then_inc(S[f"g_in{c % NG6}"], 16)

            all_tiles(sp, tile, NG6 + NU, 0)
            for c in range(NT - NG6, NT):
                moved(sp, "stored", 0, c)

        @block.tensor
        def _(pe):
            mm = nc.tensor.matmul

            def a_transpose(i):
                W(pe, "xn_ready", i + 3)
                W(pe, "lo_ready", i + 2)
                W(pe, "x2T_sb", i - 1)
                for k in range(2):
                    ins = nc.tensor.transpose(psA[:, k * P:(k + 1) * P], xn[:, k, :], ident)
                ins.then_inc(S["xnT_ps"], 1)

            def a_values(i, par):
                W(pe, "ctx_in", 16 * (i + 2))
                W(pe, "xnT_sb", i + 3)
                W(pe, "lo_ready", i + 2)
                W(pe, "x2T_sb", i - 1)
                for k in range(2):
                    ins = mm(psA[:, 256 + k * P:256 + (k + 1) * P], ctxs[:, (par + 1) % 2, k * P:(k + 1) * P], WvT[:],
                             start=True, stop=True)
                ins.then_inc(S["v_ps"], 1)

            def a_qk(i, par):
                W(pe, "ctx_in", 16 * (i + 3))
                W(pe, "xnT_sb", i + 3)
                W(pe, "v_sb", i + 2)
                mm(psA[:, 0:T], WqkT[:, 0, :], xnT[:], start=True, stop=True)
                mm(psA[:, T:2 * T], WqkT[:, 1, :], ctxs[:, par, :], start=True, stop=True).then_inc(S["qk_ps"], 1)

            def scores(n, b, k, j):
                if j == 0 and k == 0:
                    W(pe, "s_in", 32 * (n // 2 + 1) if isinstance(n, int) else 16 * n + 32)
                W(pe, "max_done", 4 * n + j - 1)
                mm(psS[j % 2][:, :], Qst[:, b, j, k * P:(k + 1) * P].bitcast(F32R),
                   Kbd[:, b, j, :, k * P:(k + 1) * P].bitcast(F32R), start=True, stop=True).then_inc(S["s_ps"], 1)

            def scores_t(n, b, k, g):
                if g == 0:
                    if k == 0:
                        W(pe, "st_in", 96 * (n // 2 + 1) if isinstance(n, int) else 48 * n + 96)
                    W(pe, "shift_in", 16 * (n + 1))
                W(pe, "exp_done", 4 * n + g - 1)
                mm(psT[g % 2][:, :], Kst[:, b, g, k * P:(k + 1) * P].bitcast(F32R),
                   Qbd[:, b, g, :, k * P:(k + 1) * P].bitcast(F32R), start=True, stop=True).then_inc(S["st_ps"], 1)

            def weighted(n, b, k, rd):
                W(pe, "exp_done", 4 * n + 2 * rd + 2)
                if rd == 0:
                    W(pe, "ot_sb", n)
                for c in range(4):
                    u = 4 * rd + c
                    ins = mm(psO[32 * c:32 * c + 32, rd * T:(rd + 1) * T],
                             Vst[:, b, k, u, :, :].rearrange("p d j -> p (d j)"),
                             Ex[:, u // 2, (u % 2) * T:(u % 2 + 1) * T], start=True, stop=True,
                             tile_position=(0, 32 * c))
                ins.then_inc(S["pv_ps"], 1)

            def out_t(n):
                W(pe, "ot_sb", n + 1)
                W(pe, "on_ready", n)
                for rd in range(2):
                    for j in range(2):
                        ins = nc.tensor.transpose(psD[:, j * T + rd * P:j * T + (rd + 1) * P],
                                                  OTs[:, rd * T + j * P:rd * T + (j + 1) * P], ident)
                ins.then_inc(S["d_ps"], 1)

            def step(i, par):
                for k in range(2):
                    n = 2 * i + k
                    b1 = (par + 1) % 2
                    exists = lambda s: not isinstance(i, int) or 0 <= n + s < NB
                    if exists(1):
                        W(pe, "c_shift", 2 * (n + 2))
                        W(pe, "oT_sb", n - 1)
                        if k:
                            W(pe, "c_pos", 4 * (i - 1))
                        nc.tensor.transpose(psM[0:2 * NH, 0:P], shift[:], ident).then_inc(S["shT_ps"], 1)
                    if exists(0):
                        scores_t(n, par, k, 0)
                        scores_t(n, par, k, 1)
                    if exists(2):
                        scores(n + 2, b1, k, 0)
                        scores(n + 2, b1, k, 1)
                    if k == 0 and on(i, 2):
                        a_transpose(i)
                    if exists(-2):
                        W(pe, "oT_sb", n - 1)
                        if exists(1):
                            W(pe, "shT_sb", n + 2)
                        mm(psM[:, 256:384], OT[:], WoT[:], start=True, stop=True).then_inc(S["f_ps"], 1)
                    if k == 1 and on(i, 2):
                        a_qk(i, par)
                    if exists(0):
                        weighted(n, par, k, 0)
                        scores_t(n, par, k, 2)
                        scores_t(n, par, k, 3)
                    if exists(2):
                        scores(n + 2, b1, k, 2)
                        scores(n + 2, b1, k, 3)
                    if exists(-1):
                        out_t(n - 1)
                    if k == 0 and on(i, 1):
                        a_values(i, par)
                    if k == 0 and on(i, -2):
                        W(pe, "x2T_sb", i - 1)
                        W(pe, "x2_ready", n - 1)
                        for kk in range(2):
                            ins = mm(psM[:, 384 + kk * NE:384 + (kk + 1) * NE], x2T[:, kk * P:(kk + 1) * P], Wr[:],
                                     start=True, stop=True)
                        ins.then_inc(S["lg_ps"], 1)
                    if k == 1 and on(i, -1):
                        W(pe, "x2n_ready", i)
                        W(pe, "lo_ready", i + 3)
                        W(pe, "v_sb", i + 2)
                        for kk in range(2):
                            ins = nc.tensor.transpose(psA[:, kk * P:(kk + 1) * P], Row[:, b1, kk, D:2 * D], ident)
                        ins.then_inc(S["x2T_ps"], 1)
                    if exists(0):
                        weighted(n, par, k, 1)
                    if k == 0 and on(i, -2):
                        W(pe, "onehot_ready", i - 1)
                        lt, one = LtOne[:, 0, :], LtOne[:, 1, :]
                        mm(psM[:, 400:408], lt, onehot[:, 0, :], start=True, stop=True)
                        mm(psM[:, 408:416], lt, onehot[:, 1, :], start=True, stop=False)
                        mm(psM[:, 408:416], one, onehot[:, 0, :], start=False, stop=True)
                        mm(psM[:, 416:424], one, onehot[:, 0, :], start=True, stop=False)
                        mm(psM[:, 416:424], one, onehot[:, 1, :], start=False, stop=True).then_inc(S["rk_ps"], 1)
                    if exists(-1):
                        W(pe, "on_ready", n)
                        W(pe, "x2_ready", n - 1)
                        if k == 0:
                            W(pe, "c_pos", 4 * (i - 1))
                        nc.tensor.transpose(psM[:, 128:256], On[:], ident).then_inc(S["e_ps"], 1)

            pe.wait_ge(S["small_in"], 16)
            pe.wait_ge(S["wqk_in"], 48)
            pe.wait_ge(S["wv_in"], 32)
            pe.wait_ge(S["wo_in"], 64)
            pe.wait_ge(S["lt_ready"], 1)
            pe.wait_ge(S["bd_zero"], 5)
            all_steps(pe, step)

            pe.wait_ge(S["c_pos"], 4 * PAIRS)

            def load(m, c):
                moved(pe, "g_in", m, c)
                W(pe, "g_sb", NG6 * m + c)
                nc.tensor.transpose(psX[:, 0:P], G[:, c % NG6, D:2 * D], ident).then_inc(S["g_ps"], 1)

            def layer1(m, c):
                t, u, b = NG6 * m + c, c % NU, c % 2
                pe.wait_ge(S["g_sb"], t + 1)
                pe.wait_ge(S["w_ready"], t + 1)
                if c >= 2:
                    pe.wait_ge(S["h1_ready"], 4 * (t - 1))
                for f in range(4):
                    ins = mm(ps1[2 * b + f // 2][:, (f % 2) * P:(f % 2 + 1) * P], Ws[:, u, f * P:(f + 1) * P],
                             GT[:, u, :], start=True, stop=True)
                    if f % 2:
                        ins.then_inc(S["l1_ps"], 1)

            def layer2(m, c):
                t, u = NG6 * m + c, c % NU
                for h in range(2):
                    if c >= 1:
                        pe.wait_ge(S["h2_ready"], 2 * (t - 1) + h + 1)
                    for f in range(4):
                        if h == 0:
                            pe.wait_ge(S["h1_ready"], 4 * t + f + 1)
                        ins = mm(ps2[h][:, 0:P], W2s[:, u, f * D2 + h * P:f * D2 + (h + 1) * P],
                                 H1[:, u, f, :], start=(f == 0), stop=(f == 3))
                    ins.then_inc(S["l2_ps"], 1)

            def layer3(m, c):
                t, u = NG6 * m + c, c % NU
                W(pe, "y_ready", t)
                for h in range(2):
                    pe.wait_ge(S["h2_ready"], 2 * t + h + 1)
                    ins = mm(psY[:, 0:D], H2[:, u, h, :], Ws[:, u, D1 + h * D:D1 + (h + 1) * D],
                             start=(h == 0), stop=(h == 1))
                ins.then_inc(S["l3_ps"], 1)

            def turn(m, c):
                layer1(m, c)
                if c >= 2:
                    layer3(m, c - 2)
                if c + 1 < NT:
                    load(m, c + 1)
                if c >= 1:
                    layer2(m, c - 1)
            load(0, 0)
            all_tiles(pe, turn, NU, NG6)
            layer3(0, NT - 2)
            layer2(0, NT - 1)
            layer3(0, NT - 1)

        @block.scalar
        def _(act):
            A = nc.scalar.activation

            def step(i, par):
                for k in range(2):
                    n = 2 * i + k
                    b1 = (par + 1) % 2
                    exists = lambda s: not isinstance(i, int) or 0 <= n + s < NB
                    if exists(-2):
                        W(act, "e_ps", n - 1)
                        W(act, "f_ps", n - 2)
                        nc.scalar.copy(OT[:], psM[:, 128:256]).then_inc(S["oT_sb"], 1)
                    if exists(1):
                        W(act, "shT_ps", n + 2)
                        W(act, "shift_in", 16 * (n + 1))
                        nc.scalar.copy(shiftT[:], psM[0:2 * NH, 0:P]).then_inc(S["shT_sb"], 1)
                    if exists(-1):
                        W(act, "pv_ps", 2 * n)
                        W(act, "d_ps", n - 1)
                        nc.scalar.copy(OTs[:], psO[:, :]).then_inc(S["ot_sb"], 1)
                    for g in range(4):
                        if exists(0):
                            W(act, "st_ps", 4 * n + g + 1)
                            W(act, "pv_ps", 2 * (n - 1) + g // 2 + 1)
                            A(Ex[:, g, :], psT[g % 2][:, :], ACT.Exp, scale=SCALE).then_inc(S["exp_done"], 1)
                        if k == 0 and g == 1 and on(i, 2):
                            W(act, "xnT_ps", i + 3)
                            W(act, "qk_ps", i + 2)
                            nc.scalar.copy(xnT[:], psA[:, 0:T]).then_inc(S["xnT_sb"], 1)
                        if k == 1 and g == 1 and on(i, 2):
                            W(act, "qk_ps", i + 3)
                            if not isinstance(i, int) or i + 1 >= 0:
                                W(act, "st_in", 96 * (i + 2))
                                W(act, "s_in", 32 * (i + 2))
                            for q in range(2):
                                A(HL[:, 2 * q, :].bitcast(F32R), psA[:, q * T:(q + 1) * T], ACT.Identity,
                                  bias=Bqk[:, q:q + 1]).then_inc(S["hi_ready"], 1)
                    if k == 1 and on(i, 2):
                        W(act, "lo_ready", i + 3)
                        for j in range(2):
                            nc.scalar.mul(HLm[:, :, 2 + j, :], HL[:, 0:3, :],
                                          C[:, C_MASK + 2 + j:C_MASK + 3 + j]).then_inc(S["masked_act"], 1)
                    if k == 1 and on(i, -1):
                        W(act, "x2T_ps", i)
                        W(act, "lg_ps", i - 1)
                        nc.scalar.copy(x2T[:], psA[:, 0:T]).then_inc(S["x2T_sb"], 1)

            act.wait_ge(S["small_in"], 16)
            act.wait_ge(S["wqk_in"], 48)
            all_steps(act, step)

            def transposed(m, c):
                t, u = NG6 * m + c, c % NU
                act.wait_ge(S["g_ps"], t + 1)
                if c >= NU:
                    act.wait_ge(S["l1_ps"], 2 * (t - NU + 1))
                nc.scalar.copy(GT[:, u, :], psX[:, 0:P]).then_inc(S["g_sb"], 1)

            def hidden1(m, c):
                t, u, b = NG6 * m + c, c % NU, c % 2
                for f in range(4):
                    if f % 2 == 0:
                        act.wait_ge(S["l1_ps"], 2 * t + f // 2 + 1)
                    if f == 0 and c >= NU:
                        act.wait_ge(S["l2_ps"], 2 * (t - NU + 1))
                    A(H1[:, u, f, :], ps1[2 * b + f // 2][:, (f % 2) * P:(f % 2 + 1) * P], ACT.Gelu,
                      bias=Ws[:, u, D1 + 2 * D + f:D1 + 2 * D + f + 1]).then_inc(S["h1_ready"], 1)

            def hidden2(m, c):
                t, u = NG6 * m + c, c % NU
                for h in range(2):
                    act.wait_ge(S["l2_ps"], 2 * t + h + 1)
                    if h == 0 and c >= NU:
                        act.wait_ge(S["l3_ps"], t - NU + 1)
                    A(H2[:, u, h, :], ps2[h][:, 0:P], ACT.Gelu,
                      bias=Ws[:, u, D1 + 2 * D + 4 + h:D1 + 2 * D + 5 + h]).then_inc(S["h2_ready"], 1)

            def turn(m, c):
                hidden1(m, c)
                if c + 1 < NT:
                    transposed(m, c + 1)
                if c >= 1:
                    hidden2(m, c - 1)

            act.wait_ge(S["tables"], 3)
            transposed(0, 0)
            all_tiles(act, turn, NU, NG6)
            hidden2(0, NT - 1)

        @block.vector
        def _(dve):
            V = nc.vector
            V.memset(Vst[:], 1.0).then_inc(S["bd_zero"], 1)
            V.memset(Kst[96:P, :, :, :], 1.0).then_inc(S["bd_zero"], 1)
            V.memset(Qbd[96:P, :, :, :, :], 0.0).then_inc(S["bd_zero"], 1)
            dve.wait_ge(S["small_in"], 16)
            V.tensor_copy(LtOne[:].rearrange("p a b -> p (a b)"), C[:, C_LT:C_LT + 2 * P]).then_inc(S["lt_ready"], 1)
            V.tensor_copy(base[:], C[:, C_REGION:C_REGION + NE]).then_inc(S["c_rk"], 1)
            dve.wait_ge(S["wqk_in"], 48)
            dve.wait_ge(S["wv_in"], 32)
            dve.wait_ge(S["wo_in"], 64)
            dve.wait_ge(S["bd_zero"], 5)

            def maxima(n, j):
                W(dve, "s_ps", 4 * n + j + 1)
                W(dve, "c_shift", 2 * n)
                V.tensor_reduce(negmax[:, 4 * j:4 * j + 4], psS[j % 2][:, :].rearrange("p (a b) -> p a b", b=P),
                                axis=AX.X, op=ALU.max, negate=True).then_inc(S["max_done"], 1)

            def shift_parts(n):
                W(dve, "max_done", 4 * n + 4)
                W(dve, "shT_ps", n)
                link = Link(dve, "c_shift", n, 2)
                link(V.tensor_copy(shift[:, 0:NH].bitcast(F32R), negmax[:]))
                link(V.tensor_tensor(shift[:, NH:2 * NH], negmax[:], shift[:, 0:NH], op=ALU.subtract))
                link.end()

            def step(i, par):
                for k in range(2):
                    n = 2 * i + k
                    b1 = (par + 1) % 2
                    exists = lambda s: not isinstance(i, int) or 0 <= n + s < NB
                    if k == 0 and on(i, 2):
                        p = i + 2
                        if isinstance(i, int):
                            W(dve, "x_in", 16 if p < 2 else 32)
                        link = Link(dve, "c_ln", p, 4)
                        W(dve, "ln_rstd", p)
                        W(dve, "xn_ready", p)
                        for kk in range(2):
                            src = X[:, 2 * p + kk, :] if isinstance(p, int) else X[:, bass.ds(2 * p + kk, 1), :].rearrange("p a b -> p (a b)")
                            link(V.bn_stats(stats[:, kk, :], src), alone=True)
                        for kk in range(2):
                            link(V.bn_aggr(mv[:, kk, :], stats[:, kk, :]), alone=True)
                        link.end()
                        V.tensor_scalar(mv[:, :, 1], mv[:, :, 1], EPS, None, op0=ALU.add).then_inc(S["ln_stats"], 1)
                    if exists(2):
                        maxima(n + 2, 0)
                        maxima(n + 2, 1)
                    if k == 0 and on(i, 2):
                        p = i + 2
                        W(dve, "ln_rstd", p + 1)
                        W(dve, "xnT_ps", p)
                        for kk in range(2):
                            src = X[:, 2 * p + kk, :] if isinstance(p, int) else X[:, bass.ds(2 * p + kk, 1), :].rearrange("p a b -> p (a b)")
                            ins = V.tensor_scalar(xn[:, kk, :], src, mv[:, kk, 0:1], rstd[:, kk:kk + 1],
                                                  op0=ALU.subtract, op1=ALU.mult)
                        ins.then_inc(S["xn_ready"], 1)
                    if exists(-2):
                        W(dve, "f_ps", n - 1)
                        W(dve, "res_ready", n - 1)
                        W(dve, "x2n_ready", i - 1)
                        link = Link(dve, "c_res", n - 2, 1)
                        V.tensor_tensor(Row[:, b1, k, 0:D], psM[:, 256:384], Row[:, b1, k, 0:D],
                                        op=ALU.add).then_inc(S["x2_ready"], 1)
                        dve.wait_ge(S["x2_ready"], n - 1)
                        link(V.bn_stats(stats2[:], Row[:, b1, k, 0:D]), alone=True)
                        link.end()
                        link = Link(dve, "c_ln2", n - 2, 1)
                        link(V.bn_aggr(mv2[:, k, :], stats2[:]))
                        link.end()
                        if k == 1:
                            V.tensor_scalar(mv2[:, :, 1], mv2[:, :, 1], EPS, None,
                                            op0=ALU.add).then_inc(S["ln2_stats"], 1)
                    if k == 1 and on(i, 2):
                        p = i + 2
                        W(dve, "hi_ready", 2 * (p + 1))
                        for q in range(2):
                            ins = V.scalar_tensor_tensor(HL[:, 2 * q + 1, :], psA[:, q * T:(q + 1) * T],
                                                         Bqk[:, q:q + 1], HL[:, 2 * q, :], op0=ALU.add,
                                                         op1=ALU.subtract)
                        ins.then_inc(S["lo_ready"], 1)
                        dve.wait_ge(S["lo_ready"], p + 1)
                        for j in range(2):
                            ins = V.tensor_scalar(HLm[:, :, j, :], HL[:, 0:3, :], C[:, C_MASK + j:C_MASK + j + 1],
                                                  None, op0=ALU.mult)
                        ins.then_inc(S["masked"], 1)
                    if exists(2):
                        maxima(n + 2, 2)
                        maxima(n + 2, 3)
                        shift_parts(n + 2)
                    if exists(-1):
                        W(dve, "d_ps", n)
                        W(dve, "e_ps", n - 1)
                        link = Link(dve, "c_norm", n - 1, 1)
                        view = psD[:, :].rearrange("p (a e) -> p a e", e=32)
                        link(V.reciprocal(rec[:], view[:, :, 2]))
                        link.end()
                        for j in range(2):
                            v = psD[:, j * T:(j + 1) * T].rearrange("p (u d e) -> p u d e", d=DH, e=4)
                            ins = V.tensor_tensor(On[:, j * 64:(j + 1) * 64].rearrange("p (u d) -> p u d", d=DH),
                                                  v[:, :, :, j],
                                                  rec[:, 8 * j:8 * j + 8].unsqueeze(2).to_broadcast([P, 8, DH]),
                                                  op=ALU.mult)
                        ins.then_inc(S["on_ready"], 1)
                    if k == 0 and on(i, 1):
                        W(dve, "v_ps", i + 2)
                        W(dve, "pv_ps", 4 * i)
                        V.tensor_tensor(Vst[:, b1, :, :, :, 0:2].rearrange("p b u d j -> p b (u d) j"),
                                        psA[:, 256:512].rearrange("p (b c j) -> p b c j", b=2, j=2),
                                        Bv[:].rearrange("p (c j) -> p c j", j=2).unsqueeze(1).to_broadcast([P, 2, 64, 2]),
                                        op=ALU.add).then_inc(S["v_sb"], 1)
                    if k == 0 and on(i, -2):
                        q = i - 2
                        W(dve, "lg_ps", q + 1)
                        W(dve, "rk_ps", q)
                        link = Link(dve, "c_lg", q, 5)
                        brb = Br[:].unsqueeze(1).to_broadcast([P, 2, NE])
                        link(V.tensor_tensor(logit[:], psM[:, 384:400].rearrange("p (k e) -> p k e", e=NE), brb,
                                             op=ALU.add))
                        link(V.tensor_reduce(best[:], logit[:], axis=AX.X, op=ALU.max))
                        link(V.tensor_tensor(pick[:], logit[:], best[:].unsqueeze(2).to_broadcast([P, 2, NE]),
                                             op=ALU.is_equal))
                        link(V.tensor_tensor(pick[:], pick[:],
                                             C[:, C_FIRST:C_FIRST + NE].unsqueeze(1).to_broadcast([P, 2, NE]),
                                             op=ALU.mult))
                        link(V.tensor_reduce(best[:], pick[:], axis=AX.X, op=ALU.max))
                        link.end()
                        V.tensor_tensor(onehot[:], pick[:], best[:].unsqueeze(2).to_broadcast([P, 2, NE]),
                                        op=ALU.is_equal).then_inc(S["onehot_ready"], 1)
                        dve.wait_ge(S["onehot_ready"], q + 1)
                        W(dve, "rk_ps", q + 1)
                        link = Link(dve, "c_pos", q, 4)
                        link(V.tensor_tensor(rank[:], psM[:, 400:416].rearrange("p (k e) -> p k e", e=NE),
                                             base[:].unsqueeze(1).to_broadcast([P, 2, NE]), op=ALU.add))
                        link(V.tensor_tensor(rank[:], rank[:], onehot[:], op=ALU.mult))
                        link(V.tensor_reduce(posf[:], rank[:], axis=AX.X, op=ALU.add))
                        link(V.tensor_tensor(base[:], psM[:, 416:424], base[:], op=ALU.add))
                        link.end()
                        V.tensor_copy(pos[:, par, :], posf[:]).then_inc(S["pos_ready"], 1)

            all_steps(dve, step)

            link = Link(dve, "c_tab", 0, 13)
            V.tensor_copy(padrow[:], base[:]).then_inc(S["tables"], 1)
            link(V.tensor_tensor(cnt[:], base[:], C[:, C_REGION:C_REGION + NE], op=ALU.subtract))
            link(V.tensor_scalar(cnti[:], cnt[:], float(P - 1), None, op0=ALU.add))
            link(V.tensor_scalar(cnti[:], cnti[:], 7, None, op0=ALU.arith_shift_right))
            link(V.tensor_copy(ntile[:], cnti[:]))
            link(V.tensor_tensor(cumw[:], C[:, C_TRI:C_TRI + 64].rearrange("p (a b) -> p a b", b=NE),
                                 ntile[:].unsqueeze(1).to_broadcast([P, NE, NE]), op=ALU.mult))
            link(V.tensor_reduce(cum[:], cumw[:], axis=AX.X, op=ALU.add))
            link(V.tensor_tensor(past[:], C[:, C_JT:C_JT + NT].unsqueeze(2).to_broadcast([P, NT, NE]),
                                 cum[:].unsqueeze(1).to_broadcast([P, NT, NE]), op=ALU.is_ge))
            link(V.tensor_reduce(texp[:], past[:], axis=AX.X, op=ALU.add))
            link(V.tensor_tensor(pastn[:], past[:], ntile[:].unsqueeze(1).to_broadcast([P, NT, NE]), op=ALU.mult))
            link(V.tensor_reduce(tdone[:], pastn[:], axis=AX.X, op=ALU.add))
            link(V.tensor_tensor(tdone[:], C[:, C_JT:C_JT + NT], tdone[:], op=ALU.subtract))
            link(V.tensor_scalar(tdone[:], tdone[:], float(P), None, op0=ALU.mult))
            link(V.scalar_tensor_tensor(tdone[:], texp[:], float(REGION), tdone[:], op0=ALU.mult, op1=ALU.add))
            link.end()
            V.tensor_scalar(wexp_i[:], texp[:], float(NE - 1), None, op0=ALU.min).then_inc(S["tables"], 1)
            V.tensor_scalar(trow_i[:], tdone[:], float(WB), None, op0=ALU.min).then_inc(S["tables"], 1)
            dve.wait_ge(S["tables"], 3)
            dve.wait_ge(S["w_in"], 48)

            def copy_weights(m, c):
                e = dve.value_load(column(wexp_i, m, c), min_val=0, max_val=NE - 1)
                if c >= NU:
                    dve.wait_ge(S["l3_ps"], NG6 * m + c - NU + 1)
                V.tensor_copy(Ws[:, c % NU, :], WAll[:, bass.ds(e, 1), :].rearrange("p a b -> p (a b)"))
                V.tensor_copy(W2s[:, c % NU, :], W2All[:, bass.ds(e, 1), :].rearrange("p a b -> p (a b)")
                              ).then_inc(S["w_ready"], 1)

            def result(m, c):
                t, u = NG6 * m + c, c % NU
                dve.wait_ge(S["l3_ps"], t + 1)
                dve.wait_ge(S["xb_ready"], t + 1)
                if c >= NU:
                    moved(dve, "stored", m, c - NU)
                V.tensor_tensor(OUT[:, u, :], psY[:, 0:D], XB[:, u, :], op=ALU.add).then_inc(S["y_ready"], 1)

            def turn(m, c):
                if c >= NU:
                    result(m, c - NU)
                copy_weights(m, c)
            all_tiles(dve, turn, NG6, NU)
            for c in range(NT - NU, NT):
                result(0, c)

        @block.gpsimd
        def _(pool):
            G_ = nc.gpsimd
            G_.memset(Qst[:], 0.0).then_inc(S["bd_zero"], 1)
            G_.memset(Kbd[:], 0.0).then_inc(S["bd_zero"], 1)
            G_.memset(PadTile[:], 0.0).then_inc(S["const_zero"], 1)
            pool.wait_ge(S["const_zero"], 1)
            G_.memset(PadTile[:, 2 * D:ROW].bitcast(I32), TOKENS).then_inc(S["const_zero"], 1)
            pool.wait_ge(S["small_in"], 16)
            pool.wait_ge(S["wo_in"], 64)
            pool.wait_ge(S["tok_in"], 16)
            pool.wait_ge(S["x_in"], 32)
            half = C[:, C_HALF:C_HALF + 2]

            def step(i, par):
                for k in range(2):
                    n = 2 * i + k
                    b1 = (par + 1) % 2
                    exists = lambda s: not isinstance(i, int) or 0 <= n + s < NB
                    if k == 0 and on(i, 2):
                        W(pool, "ln_stats", i + 3)
                        W(pool, "xn_ready", i + 2)
                        G_.tensor_tensor(rstd[:], mv[:, :, 1], half, op=ALU.pow).then_inc(S["ln_rstd"], 1)
                    if exists(-2):
                        m = n - 2
                        W(pool, "scattered", 32 * (i - 2))
                        srcx = X[:, m, :] if isinstance(m, int) else X[:, bass.ds(m, 1), :].rearrange("p a b -> p (a b)")
                        srct = Tok[:, m:m + 1] if isinstance(m, int) else Tok[:, bass.ds(m, 1)]
                        G_.tensor_copy(Row[:, b1, k, 2 * D:ROW].bitcast(I32), srct)
                        G_.tensor_tensor(Row[:, b1, k, 0:D], srcx, Bo[:], op=ALU.add).then_inc(S["res_ready"], 1)
                    if k == 1 and on(i, -1):
                        W(pool, "ln2_stats", i)
                        link = Link(pool, "c_pool", i - 1, 3)
                        link(G_.tensor_tensor(rstd2[:], mv2[:, :, 1], half, op=ALU.pow))
                        link(G_.tensor_tensor(nrm2[:], mv2[:, :, 0], rstd2[:], op=ALU.mult), alone=True)
                        link(G_.tensor_scalar(nrm2[:], nrm2[:], -1.0, 0.0, op0=ALU.mult, op1=ALU.add), alone=True)
                        link.end()
                        for kk in range(2):
                            ins = G_.tensor_scalar(Row[:, b1, kk, D:2 * D], Row[:, b1, kk, 0:D],
                                                   rstd2[:, kk:kk + 1], nrm2[:, kk:kk + 1],
                                                   op0=ALU.mult, op1=ALU.add)
                        ins.then_inc(S["x2n_ready"], 1)
                    if k == 1 and on(i, -2):
                        W(pool, "pos_ready", i - 1)
                        W(pool, "x2T_ps", i - 1)
                        for kk in range(2):
                            G_.indirect_dma_start(
                                out=scratch, out_offset=bass.IndirectOffsetOnAxis(ap=pos[:, par, kk:kk + 1], axis=0),
                                in_=Row[:, par, kk, :], in_offset=None).then_inc(S["scattered"], 16)

            all_steps(pool, step)
            W(pool, "tables", 3)
            pool.wait_ge(S["w_in"], 48)

            def residual(m, c):
                e = pool.value_load(column(wexp_i, m, c), min_val=0, max_val=NE - 1)
                moved(pool, "g_in", m, c)
                if c >= NU:
                    W(pool, "y_ready", NG6 * m + c - NU + 1)
                G_.tensor_tensor(XB[:, c % NU, :], G[:, c % NG6, 0:D],
                                 B3[:, bass.ds(e, 1), :].rearrange("p a b -> p (a b)"),
                                 op=ALU.add).then_inc(S["xb_ready"], 1)

            def store(m, c):
                W(pool, "y_ready", NG6 * m + c + 1)
                G_.indirect_dma_start(
                    out=out,
                    out_offset=bass.IndirectOffsetOnAxis(ap=G[:, c % NG6, 2 * D:ROW].bitcast(I32), axis=0),
                    in_=OUT[:, c % NU, :], in_offset=None, bounds_check=TOKENS - 1, oob_is_err=False
                ).then_inc(S[f"stored{c % NG6}"], 16)

            def turn(m, c):
                if c >= NU:
                    store(m, c - NU)
                residual(m, c)
            all_tiles(pool, turn, NU, 0)
            for c in range(NT - NU, NT):
                store(0, c)
            for c in range(NT - NG6, NT):
                moved(pool, "stored", 0, c)


def kernel(**inputs):
    import numpy as np
    import concourse.bacc as bacc
    from concourse.bass_utils import run_bass_kernel_spmd

    a = {k: np.asarray(v) for k, v in inputs.items()}
    f = np.float32
    wq = a["L0_xattn_Wq"].reshape(NG, NJ, DH, D)
    wk = a["L0_xattn_Wk"].reshape(NG, NJ, DH, D)
    wv = a["L0_xattn_Wv"].reshape(8, 2, DH, D)
    wo = a["L0_xattn_Wo"].reshape(D, 8, 2, DH)
    bq = a["L0_xattn_bq"].reshape(NG, NJ, DH)
    bk = a["L0_xattn_bk"].reshape(NG, NJ, DH)
    bv = a["L0_xattn_bv"].reshape(8, 2, DH)
    rep = lambda v: np.broadcast_to(v.reshape(1, -1), (P, v.size))
    w1 = a["L0_ffn_W1"].transpose(1, 0, 2)
    w3 = a["L0_ffn_W3"].reshape(NE, 2, P, D).transpose(2, 0, 1, 3).reshape(P, NE, 2 * D)
    b1 = a["L0_ffn_b1"].reshape(NE, 4, P).transpose(2, 0, 1)
    b2 = a["L0_ffn_b2"].reshape(NE, 2, P).transpose(2, 0, 1)
    w2 = a["L0_ffn_W2"].reshape(NE, 4, P, D2).transpose(2, 0, 1, 3).reshape(P, NE, 4 * D2)
    p = np.arange(P)
    cst = np.zeros((P, C_ALL), f)
    cst[:, C_ID:C_ID + P] = np.eye(P)
    cst[:, C_LT:C_LT + P] = p[:, None] < p[None, :]
    cst[:, C_ONE:C_ONE + P] = 1
    cst[:, C_MASK:C_MASK + NJ] = ((p[:, None] >> 2) & 3) == np.arange(NJ)
    cst[:, C_FIRST:C_FIRST + NE] = NE - np.arange(NE)
    cst[:, C_REGION:C_REGION + NE] = REGION * np.arange(NE)
    cst[:, C_TRI:C_TRI + 64] = (np.arange(NE)[None, :] <= np.arange(NE)[:, None]).reshape(1, 64)
    cst[:, C_JT:C_JT + NT] = np.arange(NT)
    cst[:, C_HALF:C_HALF + 2] = -0.5
    arrays = {
        "x": a["x"].transpose(1, 0, 2),
        "ctxT": a["ctx_1024"].transpose(2, 0, 1).reshape(D, TOKENS),
        "wqT": wq.transpose(3, 2, 1, 0).reshape(D, D),
        "wkT": wk.transpose(3, 2, 1, 0).reshape(D, D),
        "wvT": wv.transpose(3, 0, 2, 1).reshape(D, D),
        "woT": wo.transpose(2, 1, 3, 0).reshape(D, D),
        "bqk": np.stack([bq.transpose(2, 1, 0).reshape(D), bk.transpose(2, 1, 0).reshape(D)], 1),
        "bv": rep(bv.transpose(0, 2, 1)),
        "bo": rep(a["L0_xattn_bo"]),
        "wr": a["L0_ffn_Wr"],
        "br": rep(a["L0_ffn_br"]),
        "wa": np.concatenate([w1, w3, b1, b2], 2),
        "w2": w2,
        "b3": np.broadcast_to(a["L0_ffn_b3"][None], (P, NE, D)),
        "cst": cst,
        "tok": (p[:, None] + P * np.arange(NB)[None, :]).astype(np.int32),
    }
    arrays = {k: np.ascontiguousarray(v) for k, v in arrays.items()}
    nc = bacc.Bacc("TRN2", target_bir_lowering=False, num_devices=1)
    aps = {k: nc.dram_tensor(f"in_{k}", v.shape, mybir.dt.from_np(v.dtype), kind="ExternalInput").ap()
           for k, v in arrays.items()}
    out = nc.dram_tensor("out", (TOKENS, D), F32, kind="ExternalOutput").ap()
    build(nc, out=out, **aps)
    r = run_bass_kernel_spmd(nc, [{f"in_{k}": v for k, v in arrays.items()}], core_ids=[0])
    return r.results[0]["out"].reshape(NB, P, D)
```

```python
import concourse.bass as bass
from concourse import mybir
from contextlib import ExitStack

F32 = mybir.dt.float32
F32R = mybir.dt.float32r
BF16 = mybir.dt.bfloat16
I32 = mybir.dt.int32
ALU = mybir.AluOpType
ACT = mybir.ActivationFunctionType
AX = mybir.AxisListType

P = 128
D = 128
NB = 32
NH = 16
DH = 8
NG = 4
NJ = 4
PAIRS = NB // 2
T = 2 * P
NE = 8
D1, D2 = 4 * D, 2 * D
EPS = 1e-5
SCALE = DH ** -0.5
TOKENS = NB * P
REGION = TOKENS + P
ROW = 2 * D + 1
NT = NB + NE - 1
WB = NE * REGION
NU = 3
NG6 = 2 * NU
WA = D1 + 2 * D + 6

C_ID, C_LT, C_ONE, C_MASK, C_FIRST, C_REGION, C_TRI, C_JT = 0, P, 2 * P, 3 * P, 3 * P + 4, 3 * P + 12, 3 * P + 20, 3 * P + 84
C_HALF = C_JT + NT
C_TOK = C_HALF + 2
C_ALL = C_TOK + NB


def build(nc, x, ctxT, wqT, wkT, wvT, woT, bqk, bv, bo, wr, br, wa, w2, b3, cst, tok, out):
    scratch = nc.dram_tensor("scratch", (WB + P, ROW), F32, kind="Internal").ap()
    ctx = ExitStack()
    with ctx:
        def sb(name, shape, dt=F32, where=ctx):
            return where.enter_context(nc.sbuf_tensor(name, shape, dt))

        def sem(name):
            return ctx.enter_context(nc.semaphore(name))

        C = sb("C", [P, C_ALL])
        Tok = sb("Tok", [P, NB], I32)
        LtOne = sb("LtOne", [P, 2, P], BF16)
        WqkT = sb("WqkT", [P, 2, D])
        WvT = sb("WvT", [P, D])
        WoT = sb("WoT", [P, D])
        Bqk = sb("Bqk", [P, 2])
        Bv = sb("Bv", [P, D])
        Bo = sb("Bo", [P, D])
        Wr = sb("Wr", [P, NE])
        Br = sb("Br", [P, NE])
        WAll = sb("WAll", [P, NE, WA])
        W2All = sb("W2All", [P, NE, 4 * D2])
        B3 = sb("B3", [P, NE, D])
        X = sb("X", [P, NB, D])
        ident = C[:, C_ID:C_ID + P]
        stats = sb("stats", [P, 2, 6])
        mv = sb("mv", [P, 2, 2])
        rstd = sb("rstd", [P, 2])
        xn = sb("xn", [P, 2, D])
        stats2 = sb("stats2", [P, 6])
        mv2 = sb("mv2", [P, 2, 2])
        rstd2 = sb("rstd2", [P, 2])
        nrm2 = sb("nrm2", [P, 2])
        negmax = sb("negmax", [P, NH])
        shift = sb("shift", [P, 2 * NH])
        rec = sb("rec", [P, NH])
        logit = sb("logit", [P, 2, NE])
        pick = sb("pick", [P, 2, NE])
        best = sb("best", [P, 2])
        onehot = sb("onehot", [P, 2, NE], BF16)
        rank = sb("rank", [P, 2, NE])
        posf = sb("posf", [P, 2])
        pos = sb("pos", [P, 2, 2], I32)
        base = sb("base", [P, NE])
        Row = sb("Row", [P, 2, 2, ROW])
        padrow = sb("padrow", [P, NE], I32)
        PadTile = sb("PadTile", [P, ROW])
        with ExitStack() as att:
            ctxs = sb("ctxs", [P, 2, T], where=att)
            xnT = sb("xnT", [P, T], where=att)
            HL = sb("HL", [P, 4, T], where=att)
            HLm = sb("HLm", [P, 3, NJ, T], where=att)
            Qst = sb("Qst", [P, 2, NG, T], where=att)
            Kbd = sb("Kbd", [P, 2, NG, NJ, T], where=att)
            Kst = sb("Kst", [P, 2, NG, T], where=att)
            Qbd = sb("Qbd", [P, 2, NG, NJ, T], where=att)
            Vst = sb("Vst", [P, 2, 2, 8, DH, 4], where=att)
            shiftT = sb("shiftT", [2 * NH, P], where=att)
            Ex = sb("Ex", [P, NG, NJ * P], where=att)
            OTs = sb("OTs", [P, 4 * P], where=att)
            On = sb("On", [P, D], where=att)
            OT = sb("OT", [P, P], where=att)
            x2T = sb("x2T", [P, T], where=att)
        with ExitStack() as ffn:
            cnt = sb("cnt", [P, NE], where=ffn)
            cnti = sb("cnti", [P, NE], I32, where=ffn)
            ntile = sb("ntile", [P, NE], where=ffn)
            cumw = sb("cumw", [P, NE, NE], where=ffn)
            cum = sb("cum", [P, NE], where=ffn)
            past = sb("past", [P, NT, NE], where=ffn)
            pastn = sb("pastn", [P, NT, NE], where=ffn)
            texp = sb("texp", [P, NT], where=ffn)
            tdone = sb("tdone", [P, NT], where=ffn)
            wexp_i = sb("wexp_i", [P, NT], I32, where=ffn)
            trow_i = sb("trow_i", [P, NT], I32, where=ffn)
            G = sb("G", [P, 2 * NU, ROW], where=ffn)
            GT = sb("GT", [P, NU, P], where=ffn)
            Ws = sb("Ws", [P, NU, WA], where=ffn)
            W2s = sb("W2s", [P, NU, 4 * D2], where=ffn)
            H1 = sb("H1", [P, NU, 4, P], where=ffn)
            H2 = sb("H2", [P, NU, 2, P], where=ffn)
            XB = sb("XB", [P, NU, D], where=ffn)
            OUT = sb("OUT", [P, NU, D], where=ffn)

        ps = [ctx.enter_context(nc.psum_tensor(f"bank{k}", [P, 512], F32)) for k in range(8)]
        psT, psS, psO, psD, psA, psM = ps[0:2], ps[2:4], ps[4], ps[5], ps[6], ps[7]
        ps1, ps2, psY, psX = ps[0:4], ps[4:6], ps[6], ps[7]

        S = {}
        for name in """x_in ctx_in0 ctx_in1 wqk_in wv_in wo_in small_in w_in tok_in
                const_zero lt_ready bd_zero
                ln_stats ln_rstd xn_ready xnT_ps xnT_sb v_ps v_sb qk_ps hi_ready lo_ready masked masked_act
                s_in kst_in qbd_in s_ps max_done shT_ps shT_sb shift_in
                st_ps exp_done pv_ps ot_sb d_ps on_ready e_ps oT_sb f_ps bias_added x2_ready x2n_ready
                ln2_stats x2T_ps x2T_sb lg_ps onehot_ready rk_ps pos_ready scattered
                c_ln c_shift c_norm c_ln2 c_lg0 c_lg c_pos c_tab c_pool base_ready
                tables pad_in passed
                g_ps g_sb w_ready l1_ps h1_ready l2_ps h2_ready l3_ps xb_ready y_ready""".split():
            S[name] = sem(name)
        for g in range(NG6):
            S[f"g_in{g}"] = sem(f"g_in{g}")
            S[f"stored{g}"] = sem(f"stored{g}")

        def apart(eng):
            eng.sem_inc(S["passed"], 1)

        TOTAL = {"x_in": 32}
        for names, total in (("xn_ready xnT_ps xnT_sb v_ps v_sb qk_ps lo_ready masked ln_stats ln_rstd", PAIRS),
                             ("ln2_stats x2n_ready x2T_ps x2T_sb lg_ps onehot_ready rk_ps pos_ready", PAIRS),
                             ("hi_ready", 2 * PAIRS), ("masked_act", 3 * PAIRS), ("bias_added c_lg0", PAIRS), ("s_in", 32 * PAIRS),
                             ("kst_in qbd_in", 48 * PAIRS), ("shift_in scattered", 16 * NB), ("s_ps st_ps exp_done max_done", 4 * NB),
                             ("c_shift pv_ps", 2 * NB), ("c_pos", 4 * PAIRS),
                             ("shT_ps shT_sb ot_sb d_ps on_ready e_ps oT_sb f_ps x2_ready", NB)):
            for name in names.split():
                TOTAL[name] = total

        def W(eng, name, value):
            if isinstance(value, int):
                value = min(value, TOTAL.get(name, value))
                if value <= 0:
                    return
            eng.wait_ge(S[name], value)
            if not isinstance(value, int) and eng in (nc.sync, nc.gpsimd):
                apart(eng)

        class Chain:

            def __init__(self, eng, name, turn, per):
                self.eng, self.name, self.base, self.per, self.k = eng, name, turn * per, per, 0

            def did(self, ins):
                self.k += 1
                assert self.k <= self.per, self.name
                ins.then_inc(S[self.name], 1)

            def again(self, alone=False):
                value = self.base + self.k
                self.eng.wait_ge(S[self.name], value)
                if alone and not isinstance(value, int):
                    apart(self.eng)

        FIRST, LAST = -3, PAIRS + 1

        def turns_of(eng, first, stop, by):
            return eng.Fori(first, stop - by + 1, by)

        def all_steps(eng, step):
            for i in range(FIRST, 3):
                step(i, i % 2)
            with turns_of(eng, 3, PAIRS - 3, 2) as i:
                step(i, 1)
                step(i + 1, 0)
            for i in range(PAIRS - 3, LAST + 1):
                step(i, i % 2)

        def on(i, shift, lo=0, hi=PAIRS):
            return not isinstance(i, int) or lo <= i + shift < hi

        def moved(eng, name, m, c):
            eng.wait_ge(S[f"{name}{c % NG6}"], 16 * (m + c // NG6 + 1))
            if not isinstance(m, int) and eng in (nc.sync, nc.gpsimd):
                apart(eng)

        def column(table, m, c):
            return table[0:1, c:c + 1] if isinstance(m, int) else table[0:1, bass.ds(NG6 * m + c, 1)]

        def all_tiles(eng, step, head, tail):
            for c in range(head):
                step(0, c)
            with eng.Fori(0, (NT - head - tail) // NG6) as m:
                for c in range(head, head + NG6):
                    step(m, c)
            for c in range(NT - tail, NT):
                step(0, c)

        block = ctx.enter_context(nc.Block())

        @block.sync
        def _(sp):
            sp.dma_start(X[:, 0:4, :], x[:, 0:4, :]).then_inc(S["x_in"], 16)
            sp.dma_start(C[:], cst).then_inc(S["small_in"], 16)
            sp.dma_start(WqkT[:, 0, :], wqT).then_inc(S["wqk_in"], 16)
            sp.dma_start(WqkT[:, 1, :], wkT).then_inc(S["wqk_in"], 16)
            sp.dma_start(Bqk[:], bqk).then_inc(S["wqk_in"], 16)
            sp.dma_start(WvT[:], wvT).then_inc(S["wv_in"], 16)
            sp.dma_start(Bv[:], bv).then_inc(S["wv_in"], 16)
            sp.dma_start(WoT[:], woT).then_inc(S["wo_in"], 16)
            sp.dma_start(Bo[:], bo).then_inc(S["wo_in"], 16)
            sp.dma_start(Wr[:], wr).then_inc(S["wo_in"], 16)
            sp.dma_start(Br[:], br).then_inc(S["wo_in"], 16)
            sp.dma_start(Tok[:], tok).then_inc(S["tok_in"], 16)
            sp.dma_start(X[:, 4:NB, :], x[:, 4:NB, :]).then_inc(S["x_in"], 16)

            def step(i, par):
                for k in range(2):
                    n = 2 * i + k
                    if not isinstance(i, int) or 0 <= n + 1 < NB:
                        b, kk = (par + k) % 2, 1 - k
                        W(sp, "shT_sb", n + 2)
                        W(sp, "st_ps", 4 * (n - 2))
                        sp.dma_start(Qbd[96:98, b, :, :, kk * P:(kk + 1) * P].rearrange("r g j t -> r (g j) t"),
                                     shiftT[:, :]).then_inc(S["shift_in"], 16)
                    if k == 0 and on(i, 3):
                        W(sp, "qk_ps", i + 2)
                        W(sp, "v_ps", i + 2)
                        sp.dma_start(ctxs[:, (par + 1) % 2, :], ctxT[:, (i + 3) * T:(i + 4) * T] if isinstance(i, int)
                                     else ctxT[:, bass.ds((i + 3) * T, T)]).then_inc(S[f"ctx_in{(par + 1) % 2}"], 16)
                    if k == 1 and on(i, 2):
                        W(sp, "masked", i + 3)
                        W(sp, "masked_act", 3 * (i + 3))
                        W(sp, "s_ps", 8 * (i + 1))
                        if isinstance(i, int) and i == -2:
                            sp.wait_ge(S["bd_zero"], 5)
                        sp.dma_start(Qst[0:32, par, :, :], HL[:, 0, :]).then_inc(S["s_in"], 16)
                        sp.dma_start(Kbd[0:32, par, :, :, :].rearrange("r g j t -> r g (j t)"),
                                     HLm[:, 2, :, :].rearrange("p j t -> p (j t)")).then_inc(S["s_in"], 16)
                        W(sp, "st_ps", 8 * (i + 1))
                        for s, part in enumerate((2, 3, 2)):
                            sp.dma_start(Kst[32 * s:32 * s + 32, par, :, :], HL[:, part, :]).then_inc(S["kst_in"], 16)
                        for s, part in enumerate((0, 0, 1)):
                            sp.dma_start(Qbd[32 * s:32 * s + 32, par, :, :, :].rearrange("r g j t -> r g (j t)"),
                                         HLm[:, part, :, :].rearrange("p j t -> p (j t)")).then_inc(S["qbd_in"], 16)
                if not isinstance(i, int):
                    return
                if i == -2:
                    sp.dma_start(WAll[:], wa).then_inc(S["w_in"], 16)
                    sp.dma_start(B3[:], b3).then_inc(S["w_in"], 16)
                if i == -1:
                    sp.dma_start(W2All[:], w2).then_inc(S["w_in"], 16)

            all_steps(sp, step)

            sp.wait_ge(S["const_zero"], 2)
            sp.dma_start(scratch[WB:WB + P, :], PadTile[:]).then_inc(S["pad_in"], 16)
            sp.wait_ge(S["tables"], 1)
            for e in range(NE):
                r = sp.value_load(padrow[0:1, e:e + 1], min_val=0, max_val=WB - P)
                sp.dma_start(scratch[bass.ds(r, P), :], PadTile[:]).then_inc(S["pad_in"], 16)
            sp.wait_ge(S["scattered"], 16 * NB)
            sp.wait_ge(S["pad_in"], 16 * (NE + 1))
            sp.wait_ge(S["tables"], 3)

            def tile(m, c):
                if c >= NG6:
                    moved(sp, "stored", m, c - NG6)
                r = sp.value_load(column(trow_i, m, c), min_val=0, max_val=WB)
                sp.dma_start(G[:, c % NG6, :], scratch[bass.ds(r, P), :]).then_inc(S[f"g_in{c % NG6}"], 16)

            all_tiles(sp, tile, NG6 + NU, 0)
            for c in range(NT - NG6, NT):
                moved(sp, "stored", 0, c)

        @block.tensor
        def _(pe):
            mm = nc.tensor.matmul

            def a_transpose(i):
                W(pe, "xn_ready", i + 4)
                W(pe, "v_sb", i + 2)
                for k in range(2):
                    ins = nc.tensor.transpose(psA[:, k * P:(k + 1) * P], xn[:, k, :], ident)
                ins.then_inc(S["xnT_ps"], 1)

            def ctx_here(p, par):
                W(pe, f"ctx_in{par}", 8 * p + 16 - 8 * par)

            def a_qk(i, par):
                ctx_here(i + 2, par)
                W(pe, "xnT_sb", i + 3)
                W(pe, "x2T_sb", i - 1)
                mm(psA[:, 0:T], WqkT[:, 0, :], xnT[:], start=True, stop=True)
                mm(psA[:, T:2 * T], WqkT[:, 1, :], ctxs[:, par, :], start=True, stop=True).then_inc(S["qk_ps"], 1)

            def a_values(i, par):
                ctx_here(i + 1, (par + 1) % 2)
                W(pe, "lo_ready", i + 3)
                W(pe, "x2T_sb", i - 1)
                W(pe, "xnT_sb", i + 3)
                for k in range(2):
                    ins = mm(psA[:, k * P:(k + 1) * P], ctxs[:, (par + 1) % 2, k * P:(k + 1) * P], WvT[:],
                             start=True, stop=True)
                ins.then_inc(S["v_ps"], 1)

            def scores(n, b, k, j):
                if j == 0 and k == 0:
                    W(pe, "s_in", 32 * (n // 2 + 1) if isinstance(n, int) else 16 * n + 32)
                W(pe, "max_done", 4 * n + j - 1)
                mm(psS[j % 2][:, :], Qst[:, b, j, k * P:(k + 1) * P].bitcast(F32R),
                   Kbd[:, b, j, :, k * P:(k + 1) * P].bitcast(F32R), start=True, stop=True).then_inc(S["s_ps"], 1)

            def scores_t(n, b, k, g):
                if g == 0:
                    if k == 0:
                        W(pe, "kst_in", 48 * (n // 2 + 1) if isinstance(n, int) else 24 * n + 48)
                        W(pe, "qbd_in", 48 * (n // 2 + 1) if isinstance(n, int) else 24 * n + 48)
                    W(pe, "shift_in", 16 * (n + 1))
                W(pe, "exp_done", 4 * n + g - 1)
                mm(psT[g % 2][:, :], Kst[:, b, g, k * P:(k + 1) * P].bitcast(F32R),
                   Qbd[:, b, g, :, k * P:(k + 1) * P].bitcast(F32R), start=True, stop=True).then_inc(S["st_ps"], 1)

            def weighted(n, b, k, rd):
                W(pe, "exp_done", 4 * n + 2 * rd + 2)
                if rd == 0:
                    W(pe, "ot_sb", n)
                for c in range(4):
                    u = 4 * rd + c
                    ins = mm(psO[32 * c:32 * c + 32, rd * T:(rd + 1) * T],
                             Vst[:, b, k, u, :, :].rearrange("p d j -> p (d j)"),
                             Ex[:, u // 2, (u % 2) * T:(u % 2 + 1) * T], start=True, stop=True,
                             tile_position=(0, 32 * c))
                ins.then_inc(S["pv_ps"], 1)

            def out_t(n):
                W(pe, "ot_sb", n + 1)
                W(pe, "oT_sb", n)
                for rd in range(2):
                    for j in range(2):
                        ins = nc.tensor.transpose(psD[:, j * T + rd * P:j * T + (rd + 1) * P],
                                                  OTs[:, rd * T + j * P:rd * T + (j + 1) * P], ident)
                ins.then_inc(S["d_ps"], 1)

            def step(i, par):
                for k in range(2):
                    n = 2 * i + k
                    b1 = (par + 1) % 2
                    exists = lambda s: not isinstance(i, int) or 0 <= n + s < NB
                    if exists(0):
                        scores_t(n, par, k, 0)
                        scores_t(n, par, k, 1)
                    if k == 0 and on(i, -2):
                        W(pe, "x2T_sb", i - 1)
                        W(pe, "shT_sb", n + 1)
                        W(pe, "x2_ready", n - 2)
                        for kk in range(2):
                            ins = mm(psM[:, 384 + kk * NE:384 + (kk + 1) * NE], x2T[:, kk * P:(kk + 1) * P], Wr[:],
                                     start=True, stop=True)
                        ins.then_inc(S["lg_ps"], 1)
                    if exists(-2):
                        W(pe, "oT_sb", n - 1)
                        W(pe, "shT_sb", n + 1)
                        if k:
                            W(pe, "c_pos", 4 * (i - 1))
                        mm(psM[:, 256:384], OT[:], WoT[:], start=True, stop=True).then_inc(S["f_ps"], 1)
                    if exists(2):
                        scores(n + 2, b1, k, 0)
                        scores(n + 2, b1, k, 1)
                    if k == 0 and on(i, 2):
                        a_qk(i, par)
                    if exists(1):
                        W(pe, "c_shift", 2 * (n + 2))
                        W(pe, "x2_ready", n - 1)
                        if k == 0:
                            W(pe, "c_lg0", i - 1)
                        else:
                            W(pe, "c_pos", 4 * (i - 1))
                        nc.tensor.transpose(psM[0:2 * NH, 0:P], shift[:], ident).then_inc(S["shT_ps"], 1)
                    if exists(-1):
                        out_t(n - 1)
                    if exists(0):
                        weighted(n, par, k, 0)
                        scores_t(n, par, k, 2)
                        scores_t(n, par, k, 3)
                    if exists(2):
                        scores(n + 2, b1, k, 2)
                        scores(n + 2, b1, k, 3)
                    if k == 0 and on(i, 1):
                        a_values(i, par)
                    if k == 1 and on(i, 3):
                        a_transpose(i)
                    if exists(-1):
                        W(pe, "on_ready", n)
                        nc.tensor.transpose(psD[:, 0:P], On[:], ident).then_inc(S["e_ps"], 1)
                    if k == 0 and on(i, -2):
                        W(pe, "onehot_ready", i - 1)
                        W(pe, "shT_sb", n + 2)
                        W(pe, "x2_ready", n - 1)
                        lt, one = LtOne[:, 0, :], LtOne[:, 1, :]
                        mm(psM[:, 400:408], lt, onehot[:, 0, :], start=True, stop=True)
                        mm(psM[:, 408:416], lt, onehot[:, 1, :], start=True, stop=False)
                        mm(psM[:, 408:416], one, onehot[:, 0, :], start=False, stop=True)
                        mm(psM[:, 416:424], one, onehot[:, 0, :], start=True, stop=False)
                        mm(psM[:, 416:424], one, onehot[:, 1, :], start=False, stop=True).then_inc(S["rk_ps"], 1)
                    if k == 1 and on(i, -1):
                        W(pe, "x2n_ready", i)
                        W(pe, "xnT_sb", i + 4)
                        W(pe, "v_sb", i + 2)
                        for kk in range(2):
                            ins = nc.tensor.transpose(psA[:, kk * P:(kk + 1) * P], Row[:, b1, kk, D:2 * D], ident)
                        ins.then_inc(S["x2T_ps"], 1)
                    if exists(0):
                        weighted(n, par, k, 1)

            pe.wait_ge(S["small_in"], 16)
            pe.wait_ge(S["wqk_in"], 48)
            pe.wait_ge(S["wv_in"], 32)
            pe.wait_ge(S["wo_in"], 64)
            pe.wait_ge(S["lt_ready"], 1)
            pe.wait_ge(S["bd_zero"], 5)
            all_steps(pe, step)

            pe.wait_ge(S["c_pos"], 4 * PAIRS)

            def load(m, c):
                moved(pe, "g_in", m, c)
                W(pe, "g_sb", NG6 * m + c)
                nc.tensor.transpose(psX[:, 0:P], G[:, c % NG6, D:2 * D], ident).then_inc(S["g_ps"], 1)

            def layer1(m, c):
                t, u, b = NG6 * m + c, c % NU, c % 2
                pe.wait_ge(S["g_sb"], t + 1)
                pe.wait_ge(S["w_ready"], t + 1)
                if c >= 2:
                    pe.wait_ge(S["h1_ready"], 4 * (t - 1))
                for f in range(4):
                    ins = mm(ps1[2 * b + f // 2][:, (f % 2) * P:(f % 2 + 1) * P], Ws[:, u, f * P:(f + 1) * P],
                             GT[:, u, :], start=True, stop=True)
                    if f % 2:
                        ins.then_inc(S["l1_ps"], 1)

            def layer2(m, c):
                t, u = NG6 * m + c, c % NU
                for h in range(2):
                    if c >= 1:
                        pe.wait_ge(S["h2_ready"], 2 * (t - 1) + h + 1)
                    for f in range(4):
                        if h == 0:
                            pe.wait_ge(S["h1_ready"], 4 * t + f + 1)
                        ins = mm(ps2[h][:, 0:P], W2s[:, u, f * D2 + h * P:f * D2 + (h + 1) * P],
                                 H1[:, u, f, :], start=(f == 0), stop=(f == 3))
                    ins.then_inc(S["l2_ps"], 1)

            def layer3(m, c):
                t, u = NG6 * m + c, c % NU
                W(pe, "y_ready", t)
                for h in range(2):
                    pe.wait_ge(S["h2_ready"], 2 * t + h + 1)
                    ins = mm(psY[:, 0:D], H2[:, u, h, :], Ws[:, u, D1 + h * D:D1 + (h + 1) * D],
                             start=(h == 0), stop=(h == 1))
                ins.then_inc(S["l3_ps"], 1)

            def turn(m, c):
                layer1(m, c)
                if c >= 2:
                    layer3(m, c - 2)
                if c + 1 < NT:
                    load(m, c + 1)
                if c >= 1:
                    layer2(m, c - 1)
            load(0, 0)
            all_tiles(pe, turn, NU, NG6)
            layer3(0, NT - 2)
            layer2(0, NT - 1)
            layer3(0, NT - 1)

        @block.scalar
        def _(act):
            A = nc.scalar.activation

            def exponentials(n, g):
                W(act, "st_ps", 4 * n + g + 1)
                W(act, "pv_ps", 2 * (n - 1) + g // 2 + 1)
                A(Ex[:, g, :], psT[g % 2][:, :], ACT.Exp, scale=SCALE).then_inc(S["exp_done"], 1)

            def masks(i, first, stop):
                W(act, "lo_ready", i + 3)
                W(act, "qbd_in", 48 * (i + 2))
                for j in range(first, stop):
                    nc.scalar.mul(HLm[:, :, j, :], HL[:, 0:3, :],
                                  C[:, C_MASK + j:C_MASK + j + 1]).then_inc(S["masked_act"], 1)

            def step(i, par):
                for k in range(2):
                    n = 2 * i + k
                    b1 = (par + 1) % 2
                    exists = lambda s: not isinstance(i, int) or 0 <= n + s < NB
                    if exists(-1):
                        W(act, "pv_ps", 2 * n)
                        W(act, "d_ps", n - 1)
                        nc.scalar.copy(OTs[:], psO[:, :]).then_inc(S["ot_sb"], 1)
                    if exists(0):
                        exponentials(n, 0)
                        exponentials(n, 1)
                    if k == 0 and on(i, 2):
                        W(act, "qk_ps", i + 3)
                        W(act, "kst_in", 48 * (i + 2))
                        W(act, "s_in", 32 * (i + 2))
                        W(act, "masked", i + 2)
                        for q in range(2):
                            A(HL[:, 2 * q, :].bitcast(F32R), psA[:, q * T:(q + 1) * T], ACT.Identity,
                              bias=Bqk[:, q:q + 1]).then_inc(S["hi_ready"], 1)
                    if exists(1):
                        W(act, "shT_ps", n + 2)
                        W(act, "shift_in", 16 * (n + 1))
                        nc.scalar.copy(shiftT[:], psM[0:2 * NH, 0:P]).then_inc(S["shT_sb"], 1)
                    if k == 1 and on(i, 2):
                        masks(i, 3, 4)
                    if exists(0):
                        exponentials(n, 2)
                        exponentials(n, 3)
                    if k == 1 and on(i, 3):
                        W(act, "xnT_ps", i + 4)
                        W(act, "qk_ps", i + 3)
                        nc.scalar.copy(xnT[:], psA[:, 0:T]).then_inc(S["xnT_sb"], 1)
                    if k == 0 and on(i, 2):
                        masks(i, 1, 2)
                    if exists(-1):
                        W(act, "e_ps", n)
                        W(act, "f_ps", n - 1)
                        nc.scalar.copy(OT[:], psD[:, 0:P]).then_inc(S["oT_sb"], 1)
                    if k == 0 and on(i, 2):
                        masks(i, 2, 3)
                    if k == 1 and on(i, -1):
                        W(act, "x2T_ps", i)
                        W(act, "lg_ps", i - 1)
                        nc.scalar.copy(x2T[:], psA[:, 0:T]).then_inc(S["x2T_sb"], 1)

            act.wait_ge(S["small_in"], 16)
            act.wait_ge(S["wqk_in"], 48)
            all_steps(act, step)

            def transposed(m, c):
                t, u = NG6 * m + c, c % NU
                act.wait_ge(S["g_ps"], t + 1)
                if c >= NU:
                    act.wait_ge(S["l1_ps"], 2 * (t - NU + 1))
                nc.scalar.copy(GT[:, u, :], psX[:, 0:P]).then_inc(S["g_sb"], 1)

            def hidden1(m, c):
                t, u, b = NG6 * m + c, c % NU, c % 2
                for f in range(4):
                    if f % 2 == 0:
                        act.wait_ge(S["l1_ps"], 2 * t + f // 2 + 1)
                    if f == 0 and c >= NU:
                        act.wait_ge(S["l2_ps"], 2 * (t - NU + 1))
                    A(H1[:, u, f, :], ps1[2 * b + f // 2][:, (f % 2) * P:(f % 2 + 1) * P], ACT.Gelu,
                      bias=Ws[:, u, D1 + 2 * D + f:D1 + 2 * D + f + 1]).then_inc(S["h1_ready"], 1)

            def hidden2(m, c):
                t, u = NG6 * m + c, c % NU
                for h in range(2):
                    act.wait_ge(S["l2_ps"], 2 * t + h + 1)
                    if h == 0 and c >= NU:
                        act.wait_ge(S["l3_ps"], t - NU + 1)
                    A(H2[:, u, h, :], ps2[h][:, 0:P], ACT.Gelu,
                      bias=Ws[:, u, D1 + 2 * D + 4 + h:D1 + 2 * D + 5 + h]).then_inc(S["h2_ready"], 1)

            def turn(m, c):
                hidden1(m, c)
                if c + 1 < NT:
                    transposed(m, c + 1)
                if c >= 1:
                    hidden2(m, c - 1)

            act.wait_ge(S["tables"], 3)
            transposed(0, 0)
            all_tiles(act, turn, NU, NG6)
            hidden2(0, NT - 1)

        @block.vector
        def _(dve):
            V = nc.vector
            V.memset(Vst[:], 1.0).then_inc(S["bd_zero"], 1)
            V.memset(Kst[96:P, :, :, :], 1.0).then_inc(S["bd_zero"], 1)
            V.memset(Qbd[96:P, :, :, :, :], 0.0).then_inc(S["bd_zero"], 1)
            dve.wait_ge(S["small_in"], 16)
            V.tensor_copy(LtOne[:].rearrange("p a b -> p (a b)"), C[:, C_LT:C_LT + 2 * P]).then_inc(S["lt_ready"], 1)
            V.tensor_copy(base[:], C[:, C_REGION:C_REGION + NE]).then_inc(S["base_ready"], 1)
            dve.wait_ge(S["wqk_in"], 48)
            dve.wait_ge(S["wv_in"], 32)
            dve.wait_ge(S["wo_in"], 64)
            dve.wait_ge(S["bd_zero"], 5)

            def maxima(n, j):
                W(dve, "s_ps", 4 * n + j + 1)
                W(dve, "c_shift", 2 * n)
                V.tensor_reduce(negmax[:, 4 * j:4 * j + 4], psS[j % 2][:, :].rearrange("p (a b) -> p a b", b=P),
                                axis=AX.X, op=ALU.max, negate=True).then_inc(S["max_done"], 1)

            def token(m):
                return X[:, m, :] if isinstance(m, int) else X[:, bass.ds(m, 1), :].rearrange("p a b -> p (a b)")

            def slot(i, par, k):
                n = 2 * i + k
                b1 = (par + 1) % 2
                exists = lambda s: not isinstance(i, int) or 0 <= n + s < NB
                residual, nextmax, outputs = exists(-2), exists(2), exists(-1)
                router, project, values, norm = (k == 0 and on(i, -2), k == 0 and on(i, 2), k == 1 and on(i, 1),
                                                 on(i, 3))
                q, p = i - 2, i + 3
                ln2 = Chain(dve, "c_ln2", n - 2, 2)
                lg = Chain(dve, "c_lg", q, 4)
                at = Chain(dve, "c_pos", q, 4)
                ln = Chain(dve, "c_ln", p, 4)
                nrm = Chain(dve, "c_norm", n - 1, 1)
                sh = Chain(dve, "c_shift", n + 2, 2)
                both = lambda v: v.unsqueeze(1).to_broadcast([P, 2, NE])
                each = lambda v: v.unsqueeze(2).to_broadcast([P, 2, NE])
                x2 = Row[:, b1, k, 0:D]
                if residual:
                    W(dve, "f_ps", n - 1)
                    W(dve, "bias_added", i)
                    W(dve, "scattered", 32 * (i - 2))
                    V.tensor_tensor(x2, psM[:, 256:384], token(n - 2), op=ALU.add).then_inc(S["x2_ready"], 1)
                if router:
                    W(dve, "lg_ps", q + 1)
                    V.tensor_tensor(logit[:], psM[:, 384:400].rearrange("p (k e) -> p k e", e=NE), both(Br[:]),
                                    op=ALU.add).then_inc(S["c_lg0"], 1)
                if values:
                    W(dve, "v_ps", i + 2)
                    W(dve, "pv_ps", 4 * i)
                    V.tensor_tensor(Vst[:, b1, :, :, :, 0:2].rearrange("p b u d j -> p b (u d) j"),
                                    psA[:, 0:T].rearrange("p (b c j) -> p b c j", b=2, j=2),
                                    Bv[:].rearrange("p (c j) -> p c j", j=2).unsqueeze(1).to_broadcast([P, 2, 64, 2]),
                                    op=ALU.add).then_inc(S["v_sb"], 1)
                if k == 1 and norm:
                    W(dve, "ln_rstd", p + 1)
                    W(dve, "xnT_ps", p)
                    for kk in range(2):
                        ins = V.tensor_scalar(xn[:, kk, :], token(2 * p + kk), mv[:, kk, 0:1], rstd[:, kk:kk + 1],
                                              op0=ALU.subtract, op1=ALU.mult)
                    ins.then_inc(S["xn_ready"], 1)
                if nextmax:
                    maxima(n + 2, 0)
                if router:
                    W(dve, "c_lg0", q + 1)
                    lg.did(V.tensor_reduce(best[:], logit[:], axis=AX.X, op=ALU.max))
                if residual:
                    dve.wait_ge(S["x2_ready"], n - 1)
                    W(dve, "x2n_ready", i - 1)
                    if not isinstance(i, int):
                        apart(dve)
                    ln2.did(V.bn_stats(stats2[:], x2))
                if router:
                    lg.again()
                    lg.did(V.tensor_tensor(pick[:], logit[:], each(best[:]), op=ALU.is_equal))
                if nextmax:
                    maxima(n + 2, 1)
                if router:
                    lg.again()
                    lg.did(V.tensor_tensor(pick[:], pick[:], both(C[:, C_FIRST:C_FIRST + NE]), op=ALU.mult))
                if residual:
                    ln2.again(alone=True)
                    ln2.did(V.bn_aggr(mv2[:, k, :], stats2[:]))
                if router:
                    lg.again()
                    lg.did(V.tensor_reduce(best[:], pick[:], axis=AX.X, op=ALU.max))
                if outputs:
                    W(dve, "d_ps", n)
                    W(dve, "e_ps", n - 1)
                    view = psD[:, :].rearrange("p (a e) -> p a e", e=32)
                    nrm.did(V.reciprocal(rec[:], view[:, :, 2]))
                if router:
                    lg.again()
                    W(dve, "rk_ps", q)
                    V.tensor_tensor(onehot[:], pick[:], each(best[:]), op=ALU.is_equal).then_inc(S["onehot_ready"], 1)
                if residual and k == 1:
                    ln2.again()
                    V.tensor_scalar(mv2[:, :, 1], mv2[:, :, 1], EPS, None, op0=ALU.add).then_inc(S["ln2_stats"], 1)
                if outputs:
                    nrm.again()
                    for j in range(2):
                        v = psD[:, j * T:(j + 1) * T].rearrange("p (u d e) -> p u d e", d=DH, e=4)
                        ins = V.tensor_tensor(On[:, j * 64:(j + 1) * 64].rearrange("p (u d) -> p u d", d=DH),
                                              v[:, :, :, j],
                                              rec[:, 8 * j:8 * j + 8].unsqueeze(2).to_broadcast([P, 8, DH]),
                                              op=ALU.mult)
                    ins.then_inc(S["on_ready"], 1)
                if project:
                    W(dve, "hi_ready", 2 * (i + 3))
                    for h in range(2):
                        ins = V.scalar_tensor_tensor(HL[:, 2 * h + 1, :], psA[:, h * T:(h + 1) * T], Bqk[:, h:h + 1],
                                                     HL[:, 2 * h, :], op0=ALU.add, op1=ALU.subtract)
                    ins.then_inc(S["lo_ready"], 1)
                if nextmax:
                    maxima(n + 2, 2)
                    maxima(n + 2, 3)
                if k == 0 and norm:
                    if isinstance(i, int):
                        W(dve, "x_in", 16 if p < 2 else 32)
                    W(dve, "ln_rstd", p)
                    W(dve, "xn_ready", p)
                    if not isinstance(i, int):
                        apart(dve)
                    for kk in range(2):
                        ln.did(V.bn_stats(stats[:, kk, :], token(2 * p + kk)))
                if nextmax:
                    W(dve, "max_done", 4 * (n + 2) + 4)
                    W(dve, "shT_ps", n + 2)
                    sh.did(V.tensor_copy(shift[:, 0:NH].bitcast(F32R), negmax[:]))
                if k == 0 and norm:
                    ln.again(alone=True)
                    for kk in range(2):
                        ln.did(V.bn_aggr(mv[:, kk, :], stats[:, kk, :]))
                if nextmax:
                    sh.again()
                    sh.did(V.tensor_tensor(shift[:, NH:2 * NH], negmax[:], shift[:, 0:NH], op=ALU.subtract))
                if k == 0 and norm:
                    ln.again()
                    V.tensor_scalar(mv[:, :, 1], mv[:, :, 1], EPS, None, op0=ALU.add).then_inc(S["ln_stats"], 1)
                if router:
                    W(dve, "rk_ps", q + 1)
                    W(dve, "scattered", 32 * q)
                    at.did(V.tensor_tensor(rank[:], psM[:, 400:416].rearrange("p (k e) -> p k e", e=NE),
                                           both(base[:]), op=ALU.add))
                    at.again()
                    at.did(V.tensor_tensor(base[:], psM[:, 416:424], base[:], op=ALU.add))
                    at.did(V.tensor_tensor(rank[:], rank[:], onehot[:], op=ALU.mult))
                    at.again()
                    at.did(V.tensor_reduce(posf[:], rank[:], axis=AX.X, op=ALU.add))
                    at.again()
                    V.tensor_copy(pos[:, par, :], posf[:]).then_inc(S["pos_ready"], 1)

            def step(i, par):
                for k in range(2):
                    slot(i, par, k)

            all_steps(dve, step)

            tab = Chain(dve, "c_tab", 0, 13)

            def link(ins):
                tab.did(ins)
                tab.again()

            V.tensor_copy(padrow[:], base[:]).then_inc(S["tables"], 1)
            link(V.tensor_tensor(cnt[:], base[:], C[:, C_REGION:C_REGION + NE], op=ALU.subtract))
            link(V.tensor_scalar(cnti[:], cnt[:], float(P - 1), None, op0=ALU.add))
            link(V.tensor_scalar(cnti[:], cnti[:], 7, None, op0=ALU.arith_shift_right))
            link(V.tensor_copy(ntile[:], cnti[:]))
            link(V.tensor_tensor(cumw[:], C[:, C_TRI:C_TRI + 64].rearrange("p (a b) -> p a b", b=NE),
                                 ntile[:].unsqueeze(1).to_broadcast([P, NE, NE]), op=ALU.mult))
            link(V.tensor_reduce(cum[:], cumw[:], axis=AX.X, op=ALU.add))
            link(V.tensor_tensor(past[:], C[:, C_JT:C_JT + NT].unsqueeze(2).to_broadcast([P, NT, NE]),
                                 cum[:].unsqueeze(1).to_broadcast([P, NT, NE]), op=ALU.is_ge))
            link(V.tensor_reduce(texp[:], past[:], axis=AX.X, op=ALU.add))
            link(V.tensor_tensor(pastn[:], past[:], ntile[:].unsqueeze(1).to_broadcast([P, NT, NE]), op=ALU.mult))
            link(V.tensor_reduce(tdone[:], pastn[:], axis=AX.X, op=ALU.add))
            link(V.tensor_tensor(tdone[:], C[:, C_JT:C_JT + NT], tdone[:], op=ALU.subtract))
            link(V.tensor_scalar(tdone[:], tdone[:], float(P), None, op0=ALU.mult))
            link(V.scalar_tensor_tensor(tdone[:], texp[:], float(REGION), tdone[:], op0=ALU.mult, op1=ALU.add))
            V.tensor_scalar(wexp_i[:], texp[:], float(NE - 1), None, op0=ALU.min).then_inc(S["tables"], 1)
            V.tensor_scalar(trow_i[:], tdone[:], float(WB), None, op0=ALU.min).then_inc(S["tables"], 1)
            dve.wait_ge(S["tables"], 3)
            dve.wait_ge(S["w_in"], 48)

            def copy_weights(m, c):
                e = dve.value_load(column(wexp_i, m, c), min_val=0, max_val=NE - 1)
                if c >= NU:
                    dve.wait_ge(S["l3_ps"], NG6 * m + c - NU + 1)
                V.tensor_copy(Ws[:, c % NU, :], WAll[:, bass.ds(e, 1), :].rearrange("p a b -> p (a b)"))
                V.tensor_copy(W2s[:, c % NU, :], W2All[:, bass.ds(e, 1), :].rearrange("p a b -> p (a b)")
                              ).then_inc(S["w_ready"], 1)

            def result(m, c):
                t, u = NG6 * m + c, c % NU
                dve.wait_ge(S["l3_ps"], t + 1)
                dve.wait_ge(S["xb_ready"], t + 1)
                if c >= NU:
                    moved(dve, "stored", m, c - NU)
                V.tensor_tensor(OUT[:, u, :], psY[:, 0:D], XB[:, u, :], op=ALU.add).then_inc(S["y_ready"], 1)

            def turn(m, c):
                if c >= NU:
                    result(m, c - NU)
                copy_weights(m, c)
            all_tiles(dve, turn, NG6, NU)
            for c in range(NT - NU, NT):
                result(0, c)

        @block.gpsimd
        def _(pool):
            G_ = nc.gpsimd
            G_.memset(Qst[:], 0.0).then_inc(S["bd_zero"], 1)
            G_.memset(Kbd[:], 0.0).then_inc(S["bd_zero"], 1)
            G_.memset(PadTile[:], 0.0).then_inc(S["const_zero"], 1)
            pool.wait_ge(S["const_zero"], 1)
            G_.memset(PadTile[:, 2 * D:ROW].bitcast(I32), TOKENS).then_inc(S["const_zero"], 1)
            pool.wait_ge(S["small_in"], 16)
            pool.wait_ge(S["wo_in"], 64)
            pool.wait_ge(S["tok_in"], 16)
            pool.wait_ge(S["x_in"], 32)
            half = C[:, C_HALF:C_HALF + 2]

            def step(i, par):
                b1 = (par + 1) % 2
                if on(i, 2):
                    p = i + 2
                    W(pool, "xn_ready", p + 1)
                    for kk in range(2):
                        m = 2 * p + kk
                        src = X[:, m, :] if isinstance(m, int) else X[:, bass.ds(m, 1), :].rearrange("p a b -> p (a b)")
                        ins = G_.tensor_tensor(src, src, Bo[:], op=ALU.add)
                    ins.then_inc(S["bias_added"], 1)
                    W(pool, "lo_ready", i + 3)
                    W(pool, "qbd_in", 48 * (i + 2))
                    W(pool, "s_in", 32 * (i + 2))
                    G_.tensor_scalar(HLm[:, :, 0, :], HL[:, 0:3, :], C[:, C_MASK:C_MASK + 1], 0.0,
                                     op0=ALU.mult, op1=ALU.add).then_inc(S["masked"], 1)
                if on(i, 3):
                    W(pool, "ln_stats", i + 4)
                    W(pool, "xn_ready", i + 3)
                    G_.tensor_tensor(rstd[:], mv[:, :, 1], half, op=ALU.pow).then_inc(S["ln_rstd"], 1)
                if on(i, -2):
                    W(pool, "pos_ready", i - 1)
                    W(pool, "x2T_ps", i - 1)
                    for kk in range(2):
                        G_.indirect_dma_start(
                            out=scratch, out_offset=bass.IndirectOffsetOnAxis(ap=pos[:, par, kk:kk + 1], axis=0),
                            in_=Row[:, par, kk, :], in_offset=None).then_inc(S["scattered"], 16)
                if on(i, -1):
                    q = i - 1
                    W(pool, "scattered", 32 * (i - 2))
                    for kk in range(2):
                        m = 2 * q + kk
                        srct = Tok[:, m:m + 1] if isinstance(m, int) else Tok[:, bass.ds(m, 1)]
                        G_.tensor_copy(Row[:, b1, kk, 2 * D:ROW].bitcast(I32), srct)
                    W(pool, "ln2_stats", i)
                    ch = Chain(pool, "c_pool", q, 3)
                    ch.did(G_.tensor_tensor(rstd2[:], mv2[:, :, 1], half, op=ALU.pow))
                    ch.again()
                    ch.did(G_.tensor_tensor(nrm2[:], mv2[:, :, 0], rstd2[:], op=ALU.mult))
                    ch.again(alone=True)
                    ch.did(G_.tensor_scalar(nrm2[:], nrm2[:], -1.0, 0.0, op0=ALU.mult, op1=ALU.add))
                    ch.again(alone=True)
                    for kk in range(2):
                        ins = G_.tensor_scalar(Row[:, b1, kk, D:2 * D], Row[:, b1, kk, 0:D],
                                               rstd2[:, kk:kk + 1], nrm2[:, kk:kk + 1],
                                               op0=ALU.mult, op1=ALU.add)
                    ins.then_inc(S["x2n_ready"], 1)

            all_steps(pool, step)
            W(pool, "tables", 3)
            pool.wait_ge(S["w_in"], 48)

            def residual(m, c):
                e = pool.value_load(column(wexp_i, m, c), min_val=0, max_val=NE - 1)
                moved(pool, "g_in", m, c)
                if c >= NU:
                    W(pool, "y_ready", NG6 * m + c - NU + 1)
                G_.tensor_tensor(XB[:, c % NU, :], G[:, c % NG6, 0:D],
                                 B3[:, bass.ds(e, 1), :].rearrange("p a b -> p (a b)"),
                                 op=ALU.add).then_inc(S["xb_ready"], 1)

            def store(m, c):
                W(pool, "y_ready", NG6 * m + c + 1)
                G_.indirect_dma_start(
                    out=out,
                    out_offset=bass.IndirectOffsetOnAxis(ap=G[:, c % NG6, 2 * D:ROW].bitcast(I32), axis=0),
                    in_=OUT[:, c % NU, :], in_offset=None, bounds_check=TOKENS - 1, oob_is_err=False
                ).then_inc(S[f"stored{c % NG6}"], 16)

            def turn(m, c):
                if c >= NU:
                    store(m, c - NU)
                residual(m, c)
            all_tiles(pool, turn, NU, 0)
            for c in range(NT - NU, NT):
                store(0, c)
            for c in range(NT - NG6, NT):
                moved(pool, "stored", 0, c)


def kernel(**inputs):
    import numpy as np
    import concourse.bacc as bacc
    from concourse.bass_utils import run_bass_kernel_spmd

    a = {k: np.asarray(v) for k, v in inputs.items()}
    f = np.float32
    wq = a["L0_xattn_Wq"].reshape(NG, NJ, DH, D)
    wk = a["L0_xattn_Wk"].reshape(NG, NJ, DH, D)
    wv = a["L0_xattn_Wv"].reshape(8, 2, DH, D)
    wo = a["L0_xattn_Wo"].reshape(D, 8, 2, DH)
    bq = a["L0_xattn_bq"].reshape(NG, NJ, DH)
    bk = a["L0_xattn_bk"].reshape(NG, NJ, DH)
    bv = a["L0_xattn_bv"].reshape(8, 2, DH)
    rep = lambda v: np.broadcast_to(v.reshape(1, -1), (P, v.size))
    w1 = a["L0_ffn_W1"].transpose(1, 0, 2)
    w3 = a["L0_ffn_W3"].reshape(NE, 2, P, D).transpose(2, 0, 1, 3).reshape(P, NE, 2 * D)
    b1 = a["L0_ffn_b1"].reshape(NE, 4, P).transpose(2, 0, 1)
    b2 = a["L0_ffn_b2"].reshape(NE, 2, P).transpose(2, 0, 1)
    w2 = a["L0_ffn_W2"].reshape(NE, 4, P, D2).transpose(2, 0, 1, 3).reshape(P, NE, 4 * D2)
    p = np.arange(P)
    cst = np.zeros((P, C_ALL), f)
    cst[:, C_ID:C_ID + P] = np.eye(P)
    cst[:, C_LT:C_LT + P] = p[:, None] < p[None, :]
    cst[:, C_ONE:C_ONE + P] = 1
    cst[:, C_MASK:C_MASK + NJ] = ((p[:, None] >> 2) & 3) == np.arange(NJ)
    cst[:, C_FIRST:C_FIRST + NE] = NE - np.arange(NE)
    cst[:, C_REGION:C_REGION + NE] = REGION * np.arange(NE)
    cst[:, C_TRI:C_TRI + 64] = (np.arange(NE)[None, :] <= np.arange(NE)[:, None]).reshape(1, 64)
    cst[:, C_JT:C_JT + NT] = np.arange(NT)
    cst[:, C_HALF:C_HALF + 2] = -0.5
    arrays = {
        "x": a["x"].transpose(1, 0, 2),
        "ctxT": a["ctx_1024"].transpose(2, 0, 1).reshape(D, TOKENS),
        "wqT": wq.transpose(3, 2, 1, 0).reshape(D, D),
        "wkT": wk.transpose(3, 2, 1, 0).reshape(D, D),
        "wvT": wv.transpose(3, 0, 2, 1).reshape(D, D),
        "woT": wo.transpose(2, 1, 3, 0).reshape(D, D),
        "bqk": np.stack([bq.transpose(2, 1, 0).reshape(D), bk.transpose(2, 1, 0).reshape(D)], 1),
        "bv": rep(bv.transpose(0, 2, 1)),
        "bo": rep(a["L0_xattn_bo"]),
        "wr": a["L0_ffn_Wr"],
        "br": rep(a["L0_ffn_br"]),
        "wa": np.concatenate([w1, w3, b1, b2], 2),
        "w2": w2,
        "b3": np.broadcast_to(a["L0_ffn_b3"][None], (P, NE, D)),
        "cst": cst,
        "tok": (p[:, None] + P * np.arange(NB)[None, :]).astype(np.int32),
    }
    arrays = {k: np.ascontiguousarray(v) for k, v in arrays.items()}
    nc = bacc.Bacc("TRN2", target_bir_lowering=False, num_devices=1)
    aps = {k: nc.dram_tensor(f"in_{k}", v.shape, mybir.dt.from_np(v.dtype), kind="ExternalInput").ap()
           for k, v in arrays.items()}
    out = nc.dram_tensor("out", (TOKENS, D), F32, kind="ExternalOutput").ap()
    build(nc, out=out, **aps)
    r = run_bass_kernel_spmd(nc, [{f"in_{k}": v for k, v in arrays.items()}], core_ids=[0])
    return r.results[0]["out"].reshape(NB, P, D)
```

```python
import concourse.bass as bass
from concourse import mybir
from contextlib import ExitStack

F32 = mybir.dt.float32
F32R = mybir.dt.float32r
BF16 = mybir.dt.bfloat16
I32 = mybir.dt.int32
ALU = mybir.AluOpType
ACT = mybir.ActivationFunctionType
AX = mybir.AxisListType

P = 128
D = 128
NB = 32
NH = 16
DH = 8
NG = 4
NJ = 4
PAIRS = NB // 2
T = 2 * P
SEC = NJ * DH
ST = 3 * SEC + 2
NE = 8
D1, D2 = 4 * D, 2 * D
EPS = 1e-5
SCALE = DH ** -0.5
TOKENS = NB * P
REGION = TOKENS + P
ROW = 2 * D + 1
NT = NB + NE - 1
WB = NE * REGION
NU = 3
NG6 = 2 * NU
WA = D1 + 2 * D + 6

C_ID, C_LT, C_ONE, C_MASK, C_FIRST, C_REGION, C_TRI, C_JT = 0, P, 2 * P, 3 * P, 3 * P + 4, 3 * P + 12, 3 * P + 20, 3 * P + 84
C_HALF = C_JT + NT
C_TOK = C_HALF + 2
C_GROUP = C_TOK + NB
C_ROUND = C_GROUP + NG
C_ROW = C_ROUND + NE
C_ALL = C_ROW + NT


def build(nc, x, ctxT, wqT, wkT, wvT, woT, bqk, bv, bo, wr, br, wa, w2, b3, cst, tok, out):
    scratch = nc.dram_tensor("scratch", (WB + P, ROW), F32, kind="Internal").ap()
    ctx = ExitStack()
    with ctx:
        def sb(name, shape, dt=F32, where=ctx):
            return where.enter_context(nc.sbuf_tensor(name, shape, dt))

        def sem(name):
            return ctx.enter_context(nc.semaphore(name))

        C = sb("C", [P, C_ALL])
        Tok = sb("Tok", [P, NB], I32)
        LtOne = sb("LtOne", [P, 2, P], BF16)
        WqkT = sb("WqkT", [P, 2, D])
        WvT = sb("WvT", [P, D])
        WoT = sb("WoT", [P, D])
        Bqk = sb("Bqk", [P, 2])
        Bv = sb("Bv", [P, D])
        Bo = sb("Bo", [P, D])
        Wr = sb("Wr", [P, NE])
        Br = sb("Br", [P, NE])
        WAll = sb("WAll", [P, NE, WA])
        W2All = sb("W2All", [P, NE, 4 * D2])
        B3 = sb("B3", [P, NE, D])
        X = sb("X", [P, NB, D])
        ident = C[:, C_ID:C_ID + P]
        stats = sb("stats", [P, 2, 6])
        mv = sb("mv", [P, 2, 2])
        rstd = sb("rstd", [P, 2])
        xn = sb("xn", [P, 2, D])
        stats2 = sb("stats2", [P, 6])
        mv2 = sb("mv2", [P, 2, 2])
        rstd2 = sb("rstd2", [P, 2])
        nrm2 = sb("nrm2", [P, 2])
        negmax = sb("negmax", [P, NH])
        shift = sb("shift", [P, 2 * NH])
        rec = sb("rec", [P, NH])
        logit = sb("logit", [P, 2, NE])
        pick = sb("pick", [P, 2, NE])
        best = sb("best", [P, 2])
        onehot = sb("onehot", [P, 2, NE], BF16)
        rank = sb("rank", [P, 2, NE])
        posf = sb("posf", [P, 2])
        pos = sb("pos", [P, 2, 2], I32)
        base = sb("base", [P, NE])
        Row = sb("Row", [P, 2, 2, ROW])
        warm = sb("warm", [P, 1])
        padrow = sb("padrow", [P, NE], I32)
        PadTile = sb("PadTile", [P, ROW])
        with ExitStack() as att:
            ctxs = sb("ctxs", [P, 2, T], where=att)
            xnT = sb("xnT", [P, T], where=att)
            HL = sb("HL", [P, 4, T], where=att)
            HLm = sb("HLm", [P, 2, 3, NJ, T], where=att)
            Hg = sb("Hg", [P, 2, NG, T], where=att)
            Kst = sb("Kst", [ST, 2, NG, T], where=att)
            Qbd = sb("Qbd", [ST, 2, NG, NJ, T], where=att)
            Vst = sb("Vst", [P, 2, 2, 8, DH, 4], where=att)
            shiftT = sb("shiftT", [2 * NH, P], where=att)
            Ex = sb("Ex", [P, NG, NJ * P], where=att)
            OTs = sb("OTs", [P, 4 * P], where=att)
            On = sb("On", [P, D], where=att)
            OT = sb("OT", [P, P], where=att)
            x2T = sb("x2T", [P, T], where=att)
        with ExitStack() as ffn:
            skip = sb("skip", [P, NE], where=ffn)
            cnti = sb("cnti", [P, NE], I32, where=ffn)
            ntile = sb("ntile", [P, NE], where=ffn)
            cumw = sb("cumw", [P, NE, NE], where=ffn)
            cum = sb("cum", [P, NE], where=ffn)
            past = sb("past", [P, NT, NE], where=ffn)
            pastn = sb("pastn", [P, NT, NE], where=ffn)
            texp = sb("texp", [P, NT], where=ffn)
            tdone = sb("tdone", [P, NT], where=ffn)
            wexp_i = sb("wexp_i", [P, NT], I32, where=ffn)
            trow_i = sb("trow_i", [P, NT], I32, where=ffn)
            G = sb("G", [P, 2 * NU, ROW], where=ffn)
            GT = sb("GT", [P, NU, P], where=ffn)
            Ws = sb("Ws", [P, NU, WA], where=ffn)
            W2s = sb("W2s", [P, NU, 4 * D2], where=ffn)
            H1 = sb("H1", [P, NU, 4, P], where=ffn)
            H2 = sb("H2", [P, NU, 2, P], where=ffn)
            XB = sb("XB", [P, NU, D], where=ffn)
            OUT = sb("OUT", [P, NU, D], where=ffn)

        ps = [ctx.enter_context(nc.psum_tensor(f"bank{k}", [P, 512], F32)) for k in range(8)]
        psT, psS, psO, psD, psA, psM = ps[0:2], ps[2:4], ps[4], ps[5], ps[6], ps[7]
        ps1, ps2, psY, psX = ps[0:4], ps[4:6], ps[6], ps[7]

        S = {}
        for name in """x_in0 x_in1 ctx_in0 ctx_in1 wqk_in bqk_in wv_in wo_in small_in w_in tok_in
                const_zero lt_ready ones_ready
                ln_stats ln_rstd xn_ready xnT_ps xnT_sb v_ps v_sb qk_ps hi_ready lo_ready masked masked_act
                kst_in0 kst_in1 qbd_in0 qbd_in1 s_ps max_done shT_ps shT_sb shift_in
                st_ps exp_done pv_ps ot_sb d_ps on_ready e_ps oT_sb f_ps bias_added x2_ready x2n_ready
                ln2_stats ln2_rstd numbered x2T_ps x2T_sb lg_ps onehot_ready rk_ps pos_ready scattered
                c_ln c_shift c_norm c_ln2 c_lg0 c_lg c_pos c_tab base_ready
                tables pad_in passed
                g_ps g_sb w_ready w2_ready l1_ps h1_ready l2_ps h2_ready l3_ps xb_ready y_ready""".split():
            S[name] = sem(name)
        for g in range(NG6):
            S[f"g_in{g}"] = sem(f"g_in{g}")
            S[f"stored{g}"] = sem(f"stored{g}")

        def apart(eng):
            eng.sem_inc(S["passed"], 1)

        TOTAL = {}
        for names, total in (("xn_ready xnT_ps xnT_sb v_ps v_sb qk_ps lo_ready masked ln_stats ln_rstd", PAIRS),
                             ("ln2_stats ln2_rstd numbered x2n_ready x2T_ps x2T_sb lg_ps onehot_ready rk_ps pos_ready", PAIRS),
                             ("hi_ready", 2 * PAIRS), ("masked_act", 3 * PAIRS), ("bias_added c_lg0", PAIRS),
                             ("kst_in0 kst_in1 qbd_in0 qbd_in1", 24 * PAIRS), ("shift_in scattered", 16 * NB), ("s_ps st_ps exp_done max_done", 4 * NB),
                             ("c_shift pv_ps", 2 * NB), ("c_pos", 4 * PAIRS),
                             ("shT_ps shT_sb ot_sb d_ps on_ready e_ps oT_sb f_ps x2_ready", NB)):
            for name in names.split():
                TOTAL[name] = total

        def W(eng, name, value):
            if isinstance(value, int):
                value = min(value, TOTAL.get(name, value))
                if value <= 0:
                    return
            eng.wait_ge(S[name], value)
            if not isinstance(value, int) and eng in (nc.sync, nc.gpsimd):
                apart(eng)

        def of_pair(eng, name, p, par, per):
            W(eng, f"{name}{par}", per // 2 * (p + 2 - par))

        def covered(eng, name, value):
            if isinstance(value, int):
                W(eng, name, value)

        class Chain:

            def __init__(self, eng, name, turn, per):
                self.eng, self.name, self.base, self.per, self.k = eng, name, turn * per, per, 0

            def did(self, ins):
                self.k += 1
                assert self.k <= self.per, self.name
                ins.then_inc(S[self.name], 1)

            def again(self, alone=False):
                value = self.base + self.k
                self.eng.wait_ge(S[self.name], value)
                if alone and not isinstance(value, int):
                    apart(self.eng)

        FIRST, LAST = -3, PAIRS + 1

        def turns_of(eng, first, stop, by):
            return eng.Fori(first, stop - by + 1, by)

        def all_steps(eng, step):
            for i in range(FIRST, 3):
                step(i, i % 2)
            with turns_of(eng, 3, PAIRS - 3, 2) as i:
                step(i, 1)
                step(i + 1, 0)
            for i in range(PAIRS - 3, LAST + 1):
                step(i, i % 2)

        def early_norm(i):
            return isinstance(i, int) and i < 0

        def on(i, shift, lo=0, hi=PAIRS):
            return not isinstance(i, int) or lo <= i + shift < hi

        def moved(eng, name, m, c):
            eng.wait_ge(S[f"{name}{c % NG6}"], 16 * (m + c // NG6 + 1))
            if not isinstance(m, int) and eng in (nc.sync, nc.gpsimd):
                apart(eng)

        def column(table, m, c):
            return table[0:1, c:c + 1] if isinstance(m, int) else table[0:1, bass.ds(NG6 * m + c, 1)]

        def all_tiles(eng, step, head, tail):
            for c in range(head):
                step(0, c)
            with eng.Fori(0, (NT - head - tail) // NG6) as m:
                for c in range(head, head + NG6):
                    step(m, c)
            for c in range(NT - tail, NT):
                step(0, c)

        def pad(eng, experts):
            for e in experts:
                r = eng.value_load(padrow[0:1, e:e + 1], min_val=0, max_val=WB - P)
                eng.dma_start(scratch[bass.ds(r, P), :], PadTile[:]).then_inc(S["pad_in"], 16)

        block = ctx.enter_context(nc.Block())

        @block.sync
        def _(sp):
            def tokens_in(p, par):
                if isinstance(p, int):
                    dst, src = X[:, 2 * p:2 * p + 2, :], x[:, 2 * p:2 * p + 2, :]
                else:
                    dst, src = X[:, bass.ds(2 * p, 2), :], x[:, bass.ds(2 * p, 2), :]
                sp.dma_start(dst, src).then_inc(S[f"x_in{par}"], 16)

            tokens_in(0, 0)
            sp.dma_start(C[:], cst).then_inc(S["small_in"], 16)
            sp.dma_start(WqkT[:, 1, :], wkT).then_inc(S["wqk_in"], 16)
            sp.dma_start(ctxs[:, 0, :], ctxT[:, 0:T]).then_inc(S["ctx_in0"], 16)
            sp.dma_start(WqkT[:, 0, :], wqT).then_inc(S["wqk_in"], 16)
            sp.dma_start(Bqk[:], bqk).then_inc(S["bqk_in"], 16)
            tokens_in(1, 1)
            sp.dma_start(WvT[:], wvT).then_inc(S["wv_in"], 16)
            sp.dma_start(Bv[:], bv).then_inc(S["wv_in"], 16)
            sp.dma_start(WoT[:], woT).then_inc(S["wo_in"], 16)
            sp.dma_start(Bo[:], bo).then_inc(S["wo_in"], 16)
            sp.dma_start(Wr[:], wr).then_inc(S["wo_in"], 16)
            sp.dma_start(Br[:], br).then_inc(S["wo_in"], 16)
            sp.dma_start(Tok[:], tok).then_inc(S["tok_in"], 16)

            def stack(p, par, s):
                sp.dma_start(Qbd[SEC * s:SEC * (s + 1), par, :, :, :].rearrange("r g j t -> r g (j t)"),
                             HLm[:, par, (0, 0, 1)[s], :, :].rearrange("p j t -> p (j t)")
                             ).then_inc(S[f"qbd_in{par}"], 16)

            def step(i, par):
                if on(i, 3, 3):
                    tokens_in(i + 3, (par + 1) % 2)
                for k in range(2):
                    n = 2 * i + k
                    if not isinstance(i, int) or 0 <= n + 1 < NB:
                        b, kk = (par + k) % 2, 1 - k
                        W(sp, "shT_sb", n + 2)
                        W(sp, "st_ps", 4 * (n - 2))
                        sp.dma_start(Qbd[3 * SEC:ST, b, :, :, kk * P:(kk + 1) * P].rearrange("r g j t -> r (g j) t"),
                                     shiftT[:, :]).then_inc(S["shift_in"], 16)
                    if k == 0 and on(i, 1):
                        stack(i + 1, (par + 1) % 2, 1)
                        stack(i + 1, (par + 1) % 2, 2)
                    if k == 0 and on(i, 3, 1):
                        W(sp, "qk_ps", i + 2)
                        W(sp, "v_ps", i + 2)
                        sp.dma_start(ctxs[:, (par + 1) % 2, :], ctxT[:, (i + 3) * T:(i + 4) * T] if isinstance(i, int)
                                     else ctxT[:, bass.ds((i + 3) * T, T)]).then_inc(S[f"ctx_in{(par + 1) % 2}"], 16)
                    if k == 1 and on(i, 0):
                        for all_, w in ((WAll, wa), (W2All, w2)):
                            all_ = all_[:].rearrange("p e c -> p (e c)")
                            w = w.rearrange("p e c -> p (e c)")
                            c = w.shape[1] // PAIRS
                            cols = slice(c * i, c * (i + 1)) if isinstance(i, int) else bass.ds(c * i, c)
                            sp.dma_start(all_[:, cols], w[:, cols]).then_inc(S["w_in"], 16)
                    if k == 1 and on(i, 2):
                        W(sp, "lo_ready", i + 3)
                        if isinstance(i, int) and i == -2:
                            tokens_in(2, 0)
                        W(sp, "st_ps", 8 * (i + 1))
                        for s, part in enumerate((2, 3, 2)):
                            sp.dma_start(Kst[SEC * s:SEC * (s + 1), par, :, :], HL[:, part, :]).then_inc(S[f"kst_in{par}"], 16)
                        W(sp, "masked", i + 3)
                        W(sp, "masked_act", 3 * (i + 3))
                        stack(i + 2, par, 0)
                if isinstance(i, int) and i == LAST:
                    sp.dma_start(B3[:], b3).then_inc(S["w_in"], 16)

            all_steps(sp, step)

            sp.wait_ge(S["const_zero"], 2)
            sp.dma_start(scratch[WB:WB + P, :], PadTile[:]).then_inc(S["pad_in"], 16)
            sp.wait_ge(S["tables"], 1)
            pad(sp, range(0, NE // 2))
            sp.wait_ge(S["tables"], 2)
            sp.wait_ge(S["scattered"], 16 * NB)
            sp.wait_ge(S["pad_in"], 16 * (NE + 1))

            def tile(m, c):
                if c >= NG6:
                    moved(sp, "stored", m, c - NG6)
                r = sp.value_load(column(trow_i, m, c), min_val=0, max_val=WB)
                sp.dma_start(G[:, c % NG6, :], scratch[bass.ds(r, P), :]).then_inc(S[f"g_in{c % NG6}"], 16)

            all_tiles(sp, tile, NG6 + NU, 0)
            for c in range(NT - NG6, NT):
                moved(sp, "stored", 0, c)

        @block.tensor
        def _(pe):
            mm = nc.tensor.matmul

            def a_transpose(i):
                W(pe, "xn_ready", i + 4)
                covered(pe, "v_sb", i + 2)
                covered(pe, "c_pos", 4 * (i - 1))
                for k in range(2):
                    ins = nc.tensor.transpose(psA[:, k * P:(k + 1) * P], xn[:, k, :], ident)
                ins.then_inc(S["xnT_ps"], 1)

            def ctx_here(p, par):
                of_pair(pe, "ctx_in", p, par, 16)

            def keys(par):
                return mm(psA[:, T:2 * T], WqkT[:, 1, :], ctxs[:, par, :], start=True, stop=True)

            def a_qk(i, par):
                first = isinstance(i, int) and i < 0
                if not first:
                    ctx_here(i + 2, par)
                covered(pe, "xnT_sb", i + 3)
                W(pe, "x2T_sb", i - 1)
                ins = mm(psA[:, 0:T], WqkT[:, 0, :], xnT[:], start=True, stop=True)
                if not first:
                    ins = keys(par)
                ins.then_inc(S["qk_ps"], 1)

            def a_values(i, par):
                W(pe, "lo_ready", i + 3)
                covered(pe, "x2T_sb", i - 1)
                covered(pe, "xnT_sb", i + 3)
                for k in range(2):
                    ins = mm(psA[:, k * P:(k + 1) * P], ctxs[:, (par + 1) % 2, k * P:(k + 1) * P], WvT[:],
                             start=True, stop=True)
                return ins

            def scores(p, b, k, j):
                n = 2 * p + k
                if j == 0 and k == 0:
                    W(pe, "masked", p + 1)
                    W(pe, "masked_act", 3 * (p + 1))
                W(pe, "max_done", 4 * n + j - 1)
                mm(psS[j % 2][:, :], Hg[:, b, j, k * P:(k + 1) * P].bitcast(F32R),
                   HLm[:, b, 2, :, k * P:(k + 1) * P].bitcast(F32R), start=True, stop=True).then_inc(S["s_ps"], 1)

            def scores_t(i, b, k, g):
                n = 2 * i + k
                if g == 0:
                    if k == 0:
                        of_pair(pe, "kst_in", i, b, 48)
                        of_pair(pe, "qbd_in", i, b, 48)
                    W(pe, "shift_in", 16 * (n + 1))
                covered(pe, "exp_done", 4 * n + g - 1)
                mm(psT[g % 2][:, :], Kst[0:ST, b, g, k * P:(k + 1) * P].bitcast(F32R),
                   Qbd[0:ST, b, g, :, k * P:(k + 1) * P].bitcast(F32R), start=True, stop=True).then_inc(S["st_ps"], 1)

            def weighted(n, b, k, rd):
                W(pe, "exp_done", 4 * n + 2 * rd + 2)
                if rd == 0:
                    covered(pe, "ot_sb", n)
                for c in range(4):
                    u = 4 * rd + c
                    ins = mm(psO[32 * c:32 * c + 32, rd * T:(rd + 1) * T],
                             Vst[:, b, k, u, :, :].rearrange("p d j -> p (d j)"),
                             Ex[:, u // 2, (u % 2) * T:(u % 2 + 1) * T], start=True, stop=True,
                             tile_position=(0, 32 * c))
                ins.then_inc(S["pv_ps"], 1)

            def out_t(n):
                W(pe, "ot_sb", n + 1)
                covered(pe, "oT_sb", n)
                for rd in range(2):
                    for j in range(2):
                        ins = nc.tensor.transpose(psD[:, j * T + rd * P:j * T + (rd + 1) * P],
                                                  OTs[:, rd * T + j * P:rd * T + (j + 1) * P], ident)
                ins.then_inc(S["d_ps"], 1)

            def step(i, par):
                for k in range(2):
                    n = 2 * i + k
                    b1 = (par + 1) % 2
                    if isinstance(i, int) and i == FIRST and k == 0:
                        pe.wait_ge(S["wqk_in"], 32)
                    if isinstance(i, int) and i == -1 and k == 0:
                        pe.wait_ge(S["wv_in"], 32)
                        pe.wait_ge(S["wo_in"], 64)
                        pe.wait_ge(S["lt_ready"], 1)
                        pe.wait_ge(S["ones_ready"], 2)
                    exists = lambda s: not isinstance(i, int) or 0 <= n + s < NB
                    if exists(0):
                        scores_t(i, par, k, 0)
                        scores_t(i, par, k, 1)
                    if exists(-2):
                        W(pe, "oT_sb", n - 1)
                        covered(pe, "shT_sb", n + 1)
                        mm(psM[:, 256:384], OT[:], WoT[:], start=True, stop=True).then_inc(S["f_ps"], 1)
                    if exists(2):
                        scores(i + 1, b1, k, 0)
                        scores(i + 1, b1, k, 1)
                    if k == 0 and on(i, 2):
                        a_qk(i, par)
                    if k == 0 and on(i, -2):
                        covered(pe, "x2T_sb", i - 1)
                        W(pe, "x2_ready", n - 1)
                        for kk in range(2):
                            ins = mm(psM[:, 384 + kk * NE:384 + (kk + 1) * NE], x2T[:, kk * P:(kk + 1) * P], Wr[:],
                                     start=True, stop=True)
                        ins.then_inc(S["lg_ps"], 1)
                    if exists(-1):
                        out_t(n - 1)
                    if exists(0):
                        weighted(n, par, k, 0)
                    if exists(1):
                        covered(pe, "c_shift", 2 * (n + 2))
                        if k == 0:
                            covered(pe, "x2_ready", n - 1)
                        else:
                            W(pe, "x2_ready", n - 1)
                        if k == 0:
                            W(pe, "c_lg0", i - 1)
                        nc.tensor.transpose(psM[0:2 * NH, 0:P], shift[:], ident).then_inc(S["shT_ps"], 1)
                    if exists(0):
                        scores_t(i, par, k, 2)
                        scores_t(i, par, k, 3)
                    if exists(2):
                        scores(i + 1, b1, k, 2)
                        scores(i + 1, b1, k, 3)
                    if k == 0 and on(i, 1):
                        a_values(i, par).then_inc(S["v_ps"], 1)
                    if k == 0 and on(i, -2):
                        W(pe, "onehot_ready", i - 1)
                        if not on(i, 1):
                            W(pe, "x2T_sb", i - 1)
                        lt, one = LtOne[:, 0, :], LtOne[:, 1, :]
                        mm(psA[:, 256:264], lt, onehot[:, 0, :], start=True, stop=True)
                        mm(psA[:, 264:272], lt, onehot[:, 1, :], start=True, stop=False)
                        mm(psA[:, 264:272], one, onehot[:, 0, :], start=False, stop=True)
                        mm(psA[:, 272:280], one, onehot[:, 0, :], start=True, stop=False)
                        mm(psA[:, 272:280], one, onehot[:, 1, :], start=False, stop=True).then_inc(S["rk_ps"], 1)
                    if k == 1 and on(i, 3):
                        if isinstance(i, int) and i < -1:
                            ctx_here(i + 3, b1)
                            W(pe, "lo_ready", i + 3)
                            keys(b1)
                        a_transpose(i)
                    if exists(-1):
                        W(pe, "on_ready", n)
                        nc.tensor.transpose(psD[:, 0:P], On[:], ident).then_inc(S["e_ps"], 1)
                    if exists(0):
                        weighted(n, par, k, 1)
                    if k == 1 and on(i, -1):
                        W(pe, "x2n_ready", i)
                        W(pe, "xnT_sb", i + 4)
                        covered(pe, "v_sb", i + 2)
                        covered(pe, "c_pos", 4 * (i - 1))
                        for kk in range(2):
                            ins = nc.tensor.transpose(psA[:, kk * P:(kk + 1) * P], Row[:, b1, kk, D:2 * D], ident)
                        ins.then_inc(S["x2T_ps"], 1)

            pe.wait_ge(S["small_in"], 16)
            all_steps(pe, step)

            pe.wait_ge(S["c_pos"], 4 * PAIRS)

            def load(m, c):
                moved(pe, "g_in", m, c)
                W(pe, "g_sb", NG6 * m + c)
                nc.tensor.transpose(psX[:, 0:P], G[:, c % NG6, D:2 * D], ident).then_inc(S["g_ps"], 1)

            def layer1(m, c):
                t, u, b = NG6 * m + c, c % NU, c % 2
                pe.wait_ge(S["g_sb"], t + 1)
                pe.wait_ge(S["w_ready"], t + 1)
                if c >= 2:
                    pe.wait_ge(S["h1_ready"], 4 * (t - 1))
                for f in range(4):
                    ins = mm(ps1[2 * b + f // 2][:, (f % 2) * P:(f % 2 + 1) * P], Ws[:, u, f * P:(f + 1) * P],
                             GT[:, u, :], start=True, stop=True)
                    if f % 2:
                        ins.then_inc(S["l1_ps"], 1)

            def layer2(m, c):
                t, u = NG6 * m + c, c % NU
                pe.wait_ge(S["w2_ready"], t + 1)
                for h in range(2):
                    if c >= 1:
                        pe.wait_ge(S["h2_ready"], 2 * (t - 1) + h + 1)
                    for f in range(4):
                        if h == 0:
                            pe.wait_ge(S["h1_ready"], 4 * t + f + 1)
                        ins = mm(ps2[h][:, 0:P], W2s[:, u, f * D2 + h * P:f * D2 + (h + 1) * P],
                                 H1[:, u, f, :], start=(f == 0), stop=(f == 3))
                    ins.then_inc(S["l2_ps"], 1)

            def layer3(m, c):
                t, u = NG6 * m + c, c % NU
                W(pe, "y_ready", t)
                for h in range(2):
                    pe.wait_ge(S["h2_ready"], 2 * t + h + 1)
                    ins = mm(psY[:, 0:D], H2[:, u, h, :], Ws[:, u, D1 + h * D:D1 + (h + 1) * D],
                             start=(h == 0), stop=(h == 1))
                ins.then_inc(S["l3_ps"], 1)

            def turn(m, c):
                layer1(m, c)
                if c >= 2:
                    layer3(m, c - 2)
                if c + 1 < NT:
                    load(m, c + 1)
                if c >= 1:
                    layer2(m, c - 1)
            load(0, 0)
            all_tiles(pe, turn, NU, NG6)
            layer3(0, NT - 2)
            layer2(0, NT - 1)
            layer3(0, NT - 1)

        @block.scalar
        def _(act):
            A = nc.scalar.activation

            def exponentials(n, g):
                W(act, "st_ps", 4 * n + g + 1)
                covered(act, "pv_ps", 2 * (n - 1) + g // 2 + 1)
                A(Ex[:, g, :], psT[g % 2][:, :], ACT.Exp, scale=SCALE).then_inc(S["exp_done"], 1)

            def masks(i, par, first, stop):
                W(act, "lo_ready", i + 3)
                if isinstance(i, int):
                    of_pair(act, "qbd_in", i, par, 48)
                    W(act, "s_ps", 8 * (i + 1))
                for j in range(first, stop):
                    nc.scalar.mul(HLm[:, par, :, j, :].bitcast(F32R), HL[:, 0:3, :],
                                  C[:, C_MASK + j:C_MASK + j + 1]).then_inc(S["masked_act"], 1)

            def step(i, par):
                for k in range(2):
                    n = 2 * i + k
                    b1 = (par + 1) % 2
                    exists = lambda s: not isinstance(i, int) or 0 <= n + s < NB
                    if exists(-1):
                        W(act, "pv_ps", 2 * n)
                        covered(act, "d_ps", n - 1)
                        nc.scalar.copy(OTs[:], psO[:, :]).then_inc(S["ot_sb"], 1)
                    if exists(0):
                        exponentials(n, 0)
                        exponentials(n, 1)
                    if k == 0 and on(i, 2):
                        W(act, "qk_ps", i + 3)
                        of_pair(act, "kst_in", i + 1, (par + 1) % 2, 48)
                        covered(act, "masked", i + 2)
                        for q in range(2):
                            A(HL[:, 2 * q, :].bitcast(F32R), psA[:, q * T:(q + 1) * T], ACT.Identity,
                              bias=Bqk[:, q:q + 1]).then_inc(S["hi_ready"], 1)
                    if exists(1):
                        W(act, "shT_ps", n + 2)
                        covered(act, "shift_in", 16 * (n + 1))
                        nc.scalar.copy(shiftT[:], psM[0:2 * NH, 0:P]).then_inc(S["shT_sb"], 1)
                    if k == 1 and on(i, 2):
                        masks(i, par, 3, 4)
                    if exists(0):
                        exponentials(n, 2)
                        exponentials(n, 3)
                    if k == 1 and on(i, 3):
                        W(act, "xnT_ps", i + 4)
                        covered(act, "qk_ps", i + 3)
                        nc.scalar.copy(xnT[:], psA[:, 0:T]).then_inc(S["xnT_sb"], 1)
                    if k == 0 and on(i, 2):
                        masks(i, par, 1, 2)
                    if exists(-1):
                        W(act, "e_ps", n)
                        covered(act, "f_ps", n - 1)
                        nc.scalar.copy(OT[:], psD[:, 0:P]).then_inc(S["oT_sb"], 1)
                    if k == 0 and on(i, 2):
                        masks(i, par, 2, 3)
                    if k == 1 and on(i, -1):
                        W(act, "x2T_ps", i)
                        covered(act, "lg_ps", i - 1)
                        nc.scalar.copy(x2T[:], psA[:, 0:T]).then_inc(S["x2T_sb"], 1)

            act.wait_ge(S["small_in"], 16)
            nc.scalar.copy(LtOne[:].rearrange("p a b -> p (a b)"), C[:, C_LT:C_LT + 2 * P]).then_inc(S["lt_ready"], 1)
            act.wait_ge(S["bqk_in"], 16)
            all_steps(act, step)

            def transposed(m, c):
                t, u = NG6 * m + c, c % NU
                act.wait_ge(S["g_ps"], t + 1)
                if c >= NU:
                    act.wait_ge(S["l1_ps"], 2 * (t - NU + 1))
                nc.scalar.copy(GT[:, u, :], psX[:, 0:P]).then_inc(S["g_sb"], 1)

            def hidden1(m, c):
                t, u, b = NG6 * m + c, c % NU, c % 2
                for f in range(4):
                    if f % 2 == 0:
                        act.wait_ge(S["l1_ps"], 2 * t + f // 2 + 1)
                    if f == 0 and c >= NU:
                        act.wait_ge(S["l2_ps"], 2 * (t - NU + 1))
                    A(H1[:, u, f, :], ps1[2 * b + f // 2][:, (f % 2) * P:(f % 2 + 1) * P], ACT.Gelu,
                      bias=Ws[:, u, D1 + 2 * D + f:D1 + 2 * D + f + 1]).then_inc(S["h1_ready"], 1)

            def hidden2(m, c):
                t, u = NG6 * m + c, c % NU
                for h in range(2):
                    act.wait_ge(S["l2_ps"], 2 * t + h + 1)
                    if h == 0 and c >= NU:
                        act.wait_ge(S["l3_ps"], t - NU + 1)
                    A(H2[:, u, h, :], ps2[h][:, 0:P], ACT.Gelu,
                      bias=Ws[:, u, D1 + 2 * D + 4 + h:D1 + 2 * D + 5 + h]).then_inc(S["h2_ready"], 1)

            def turn(m, c):
                hidden1(m, c)
                if c + 1 < NT:
                    transposed(m, c + 1)
                if c >= 1:
                    hidden2(m, c - 1)

            A(warm[:], C[:, C_HALF:C_HALF + 1], ACT.Gelu).then_inc(S["passed"], 1)
            act.wait_ge(S["const_zero"], 2)
            act.wait_ge(S["tables"], 1)
            pad(act, range(NE // 2, NE))
            act.wait_ge(S["tables"], 3)
            transposed(0, 0)
            all_tiles(act, turn, NU, NG6)
            hidden2(0, NT - 1)

        @block.vector
        def _(dve):
            V = nc.vector

            def maxima(n, j):
                if isinstance(n, int) and n == 0 and j == 0:
                    dve.wait_ge(S["small_in"], 16)
                    V.tensor_copy(base[:], C[:, C_REGION:C_REGION + NE]).then_inc(S["base_ready"], 1)
                    dve.wait_ge(S["base_ready"], 1)
                W(dve, "s_ps", 4 * n + j + 1)
                if j == 0:
                    W(dve, "c_shift", 2 * n)
                V.tensor_reduce(negmax[:, 4 * j:4 * j + 4], psS[j % 2][:, :].rearrange("p (a b) -> p a b", b=P),
                                axis=AX.X, op=ALU.max, negate=True).then_inc(S["max_done"], 1)

            def token(m):
                return X[:, m, :] if isinstance(m, int) else X[:, bass.ds(m, 1), :].rearrange("p a b -> p (a b)")

            def slot(i, par, k):
                n = 2 * i + k
                b1 = (par + 1) % 2
                exists = lambda s: not isinstance(i, int) or 0 <= n + s < NB
                residual, nextmax, outputs = exists(-2), exists(2), exists(-1)
                router, project, values, norm = (k == 0 and on(i, -2), k == 0 and on(i, 2), k == 1 and on(i, 1),
                                                 on(i, 3))
                q, p = i - 2, i + 3
                ln2 = Chain(dve, "c_ln2", n - 2, 2)
                lg = Chain(dve, "c_lg", q, 4)
                at = Chain(dve, "c_pos", q, 4)
                ln = Chain(dve, "c_ln", p, 4)
                nrm = Chain(dve, "c_norm", n - 1, 1)
                sh = Chain(dve, "c_shift", n + 2, 2)
                both = lambda v: v.unsqueeze(1).to_broadcast([P, 2, NE])
                each = lambda v: v.unsqueeze(2).to_broadcast([P, 2, NE])
                x2 = Row[:, b1, k, 0:D]
                early = early_norm(i) and k == 0 and norm

                def sums():
                    of_pair(dve, "x_in", p, b1, 16)
                    covered(dve, "ln_rstd", p)
                    covered(dve, "xn_ready", p)
                    if not isinstance(i, int):
                        apart(dve)
                    for kk in range(2):
                        ln.did(V.bn_stats(stats[:, kk, :], token(2 * p + kk)))

                def means():
                    ln.again(alone=True)
                    for kk in range(2):
                        ln.did(V.bn_aggr(mv[:, kk, :], stats[:, kk, :]))

                def variances():
                    ln.again()
                    V.tensor_scalar(mv[:, :, 1], mv[:, :, 1], EPS, None, op0=ALU.add).then_inc(S["ln_stats"], 1)

                if isinstance(i, int) and i == -2 and k == 0:
                    dve.wait_ge(S["bqk_in"], 16)
                if isinstance(i, int) and i == -1 and k == 0:
                    dve.wait_ge(S["wv_in"], 32)
                    dve.wait_ge(S["wo_in"], 64)
                    dve.wait_ge(S["ones_ready"], 2)
                if residual:
                    W(dve, "f_ps", n - 1)
                    covered(dve, "bias_added", i)
                    W(dve, "scattered", 32 * (i - 2))
                    V.tensor_tensor(x2, psM[:, 256:384], token(n - 2), op=ALU.add).then_inc(S["x2_ready"], 1)
                if values:
                    covered(dve, "v_ps", i + 2)
                    covered(dve, "rk_ps", i - 1)
                    covered(dve, "pv_ps", 4 * i)
                    V.tensor_tensor(Vst[:, b1, :, :, :, 0:2].rearrange("p b u d j -> p b (u d) j"),
                                    psA[:, 0:T].rearrange("p (b c j) -> p b c j", b=2, j=2),
                                    Bv[:].rearrange("p (c j) -> p c j", j=2).unsqueeze(1).to_broadcast([P, 2, 64, 2]),
                                    op=ALU.add).then_inc(S["v_sb"], 1)
                if k == 1 and norm:
                    W(dve, "ln_rstd", p + 1)
                    covered(dve, "xnT_ps", p)
                    for kk in range(2):
                        ins = V.tensor_scalar(xn[:, kk, :], token(2 * p + kk), mv[:, kk, 0:1], rstd[:, kk:kk + 1],
                                              op0=ALU.subtract, op1=ALU.mult)
                    ins.then_inc(S["xn_ready"], 1)
                if nextmax:
                    maxima(n + 2, 0)
                if residual:
                    dve.wait_ge(S["x2_ready"], n - 1)
                    if not isinstance(i, int):
                        apart(dve)
                    ln2.did(V.bn_stats(stats2[:], x2))
                if nextmax:
                    maxima(n + 2, 1)
                if router:
                    W(dve, "lg_ps", q + 1)
                    V.tensor_tensor(logit[:], psM[:, 384:400].rearrange("p (k e) -> p k e", e=NE), both(Br[:]),
                                    op=ALU.add).then_inc(S["c_lg0"], 1)
                if residual:
                    ln2.again(alone=True)
                    ln2.did(V.bn_aggr(mv2[:, k, :], stats2[:]))
                if router:
                    W(dve, "c_lg0", q + 1)
                    lg.did(V.tensor_reduce(best[:], logit[:], axis=AX.X, op=ALU.max))
                if outputs:
                    W(dve, "d_ps", n)
                    covered(dve, "e_ps", n - 1)
                    view = psD[:, :].rearrange("p (a e) -> p a e", e=32)
                    nrm.did(V.reciprocal(rec[:], view[:, :, 2]))
                if residual and k == 1:
                    ln2.again()
                    V.tensor_scalar(mv2[:, :, 1], mv2[:, :, 1], EPS, None, op0=ALU.add).then_inc(S["ln2_stats"], 1)
                if router:
                    lg.again()
                    lg.did(V.tensor_tensor(pick[:], logit[:], each(best[:]), op=ALU.is_equal))
                if outputs:
                    nrm.again()
                    for j in range(2):
                        v = psD[:, j * T:(j + 1) * T].rearrange("p (u d e) -> p u d e", d=DH, e=4)
                        ins = V.tensor_tensor(On[:, j * 64:(j + 1) * 64].rearrange("p (u d) -> p u d", d=DH),
                                              v[:, :, :, j],
                                              rec[:, 8 * j:8 * j + 8].unsqueeze(2).to_broadcast([P, 8, DH]),
                                              op=ALU.mult)
                    ins.then_inc(S["on_ready"], 1)
                if router:
                    lg.again()
                    lg.did(V.tensor_tensor(pick[:], pick[:], both(C[:, C_FIRST:C_FIRST + NE]), op=ALU.mult))
                if early:
                    sums()
                    means()
                    variances()
                if project:
                    W(dve, "hi_ready", 2 * (i + 3))
                    for h in range(2):
                        ins = V.scalar_tensor_tensor(HL[:, 2 * h + 1, :], psA[:, h * T:(h + 1) * T], Bqk[:, h:h + 1],
                                                     HL[:, 2 * h, :], op0=ALU.add, op1=ALU.subtract)
                    ins.then_inc(S["lo_ready"], 1)
                if router:
                    lg.again()
                    lg.did(V.tensor_reduce(best[:], pick[:], axis=AX.X, op=ALU.max))
                if nextmax:
                    maxima(n + 2, 2)
                if router:
                    lg.again()
                    covered(dve, "rk_ps", q)
                    V.tensor_tensor(onehot[:], pick[:], each(best[:]), op=ALU.is_equal).then_inc(S["onehot_ready"], 1)
                if k == 1 and on(i, -1):
                    W(dve, "ln2_rstd", i)
                    for kk in range(2):
                        ins = V.tensor_scalar(Row[:, b1, kk, D:2 * D], Row[:, b1, kk, 0:D], mv2[:, kk, 0:1],
                                              rstd2[:, kk:kk + 1], op0=ALU.subtract, op1=ALU.mult)
                    ins.then_inc(S["x2n_ready"], 1)
                if nextmax:
                    maxima(n + 2, 3)
                if k == 0 and norm and not early:
                    sums()
                if router:
                    W(dve, "rk_ps", q + 1)
                    covered(dve, "scattered", 32 * q)
                    at.did(V.tensor_tensor(rank[:], psA[:, 256:272].rearrange("p (k e) -> p k e", e=NE),
                                           both(base[:]), op=ALU.add))
                if nextmax:
                    W(dve, "max_done", 4 * (n + 2) + 4)
                    covered(dve, "shT_ps", n + 2)
                    sh.did(V.tensor_copy(shift[:, 0:NH].bitcast(F32R), negmax[:]))
                if router:
                    at.again()
                    at.did(V.tensor_tensor(base[:], psA[:, 272:280], base[:], op=ALU.add))
                    if isinstance(i, int) and i == LAST:
                        at.again()
                        V.tensor_copy(padrow[:], base[:]).then_inc(S["tables"], 1)
                if k == 0 and norm and not early:
                    means()
                if router:
                    at.did(V.tensor_tensor(rank[:], rank[:], onehot[:], op=ALU.mult))
                if nextmax:
                    sh.again()
                    sh.did(V.tensor_tensor(shift[:, NH:2 * NH], negmax[:], shift[:, 0:NH], op=ALU.subtract))
                if k == 0 and norm and not early:
                    variances()
                if router:
                    at.again()
                    at.did(V.tensor_reduce(posf[:], rank[:], axis=AX.X, op=ALU.add))
                    at.again()
                    V.tensor_copy(pos[:, par, :], posf[:]).then_inc(S["pos_ready"], 1)

            def step(i, par):
                for k in range(2):
                    slot(i, par, k)

            all_steps(dve, step)

            tab = Chain(dve, "c_tab", 0, 11)

            def link(ins):
                tab.did(ins)
                tab.again()

            link(V.tensor_tensor(cnti[:], base[:], C[:, C_ROUND:C_ROUND + NE], op=ALU.subtract))
            link(V.tensor_scalar(cnti[:], cnti[:], 7, None, op0=ALU.arith_shift_right))
            link(V.tensor_copy(ntile[:], cnti[:]))
            tab.did(V.tensor_scalar(skip[:], ntile[:], -float(P), float(REGION), op0=ALU.mult, op1=ALU.add))
            link(V.tensor_tensor(cumw[:], C[:, C_TRI:C_TRI + 64].rearrange("p (a b) -> p a b", b=NE),
                                 ntile[:].unsqueeze(1).to_broadcast([P, NE, NE]), op=ALU.mult))
            link(V.tensor_reduce(cum[:], cumw[:], axis=AX.X, op=ALU.add))
            link(V.tensor_tensor(past[:], C[:, C_JT:C_JT + NT].unsqueeze(2).to_broadcast([P, NT, NE]),
                                 cum[:].unsqueeze(1).to_broadcast([P, NT, NE]), op=ALU.is_ge))
            link(V.tensor_tensor(pastn[:], past[:], skip[:].unsqueeze(1).to_broadcast([P, NT, NE]), op=ALU.mult))
            link(V.tensor_reduce(tdone[:], pastn[:], axis=AX.X, op=ALU.add))
            link(V.tensor_tensor(tdone[:], C[:, C_ROW:C_ROW + NT], tdone[:], op=ALU.add))
            V.tensor_scalar(trow_i[:], tdone[:], float(WB), None, op0=ALU.min).then_inc(S["tables"], 1)
            link(V.tensor_reduce(texp[:], past[:], axis=AX.X, op=ALU.add))
            V.tensor_scalar(wexp_i[:], texp[:], float(NE - 1), None, op0=ALU.min).then_inc(S["tables"], 1)
            dve.wait_ge(S["tables"], 3)
            dve.wait_ge(S["w_in"], 16 * (2 * PAIRS + 1))

            def copy_outer(m, c, e):
                if c >= NU:
                    dve.wait_ge(S["l3_ps"], NG6 * m + c - NU + 1)
                V.tensor_copy(Ws[:, c % NU, :], WAll[:, bass.ds(e, 1), :].rearrange("p a b -> p (a b)")
                              ).then_inc(S["w_ready"], 1)

            def copy_inner(m, c, e):
                if c >= NU:
                    dve.wait_ge(S["l2_ps"], 2 * (NG6 * m + c - NU + 1))
                V.tensor_copy(W2s[:, c % NU, :], W2All[:, bass.ds(e, 1), :].rearrange("p a b -> p (a b)")
                              ).then_inc(S["w2_ready"], 1)

            def result(m, c):
                t, u = NG6 * m + c, c % NU
                dve.wait_ge(S["l3_ps"], t + 1)
                dve.wait_ge(S["xb_ready"], t + 1)
                if c >= NU:
                    moved(dve, "stored", m, c - NU)
                V.tensor_tensor(OUT[:, u, :], psY[:, 0:D], XB[:, u, :], op=ALU.add).then_inc(S["y_ready"], 1)

            def turn(m, c):
                e = dve.value_load(column(wexp_i, m, c), min_val=0, max_val=NE - 1)
                copy_outer(m, c, e)
                if c >= NU:
                    result(m, c - NU)
                copy_inner(m, c, e)
            all_tiles(dve, turn, NG6, NU)
            for c in range(NT - NU, NT):
                result(0, c)

        @block.gpsimd
        def _(pool):
            G_ = nc.gpsimd
            G_.memset(Kst[3 * SEC:ST, :, :, :], 1.0).then_inc(S["ones_ready"], 1)
            pool.wait_ge(S["ones_ready"], 1)
            G_.memset(Vst[:], 1.0).then_inc(S["ones_ready"], 1)
            pool.wait_ge(S["ones_ready"], 2)
            G_.memset(PadTile[:], 0.0).then_inc(S["const_zero"], 1)
            pool.wait_ge(S["const_zero"], 1)
            G_.memset(PadTile[:, 2 * D:ROW].bitcast(I32), TOKENS).then_inc(S["const_zero"], 1)
            pool.wait_ge(S["small_in"], 16)
            half = C[:, C_HALF:C_HALF + 2]

            def step(i, par):
                b1 = (par + 1) % 2

                def norm_factor():
                    W(pool, "ln_stats", i + 4)
                    covered(pool, "xn_ready", i + 3)
                    G_.tensor_tensor(rstd[:], mv[:, :, 1], half, op=ALU.pow).then_inc(S["ln_rstd"], 1)

                def bias():
                    if isinstance(i, int) and i == -2:
                        pool.wait_ge(S["wo_in"], 64)
                        pool.wait_ge(S["tok_in"], 16)
                    p = i + 2
                    W(pool, "xn_ready", p + 1)
                    for kk in range(2):
                        m = 2 * p + kk
                        src = X[:, m, :] if isinstance(m, int) else X[:, bass.ds(m, 1), :].rearrange("p a b -> p (a b)")
                        ins = G_.tensor_tensor(src, src, Bo[:], op=ALU.add)
                    ins.then_inc(S["bias_added"], 1)

                def rows():
                    W(pool, "pos_ready", i - 1)
                    covered(pool, "x2n_ready", i - 1)
                    W(pool, "numbered", i - 1)
                    covered(pool, "x2T_ps", i - 1)
                    for kk in range(2):
                        G_.indirect_dma_start(
                            out=scratch, out_offset=bass.IndirectOffsetOnAxis(ap=pos[:, par, kk:kk + 1], axis=0),
                            in_=Row[:, par, kk, :], in_offset=None).then_inc(S["scattered"], 16)

                rows_last = isinstance(i, int) and i == LAST - 1
                if on(i, 3) and early_norm(i):
                    norm_factor()
                if on(i, 2):
                    if not early_norm(i):
                        bias()
                    W(pool, "hi_ready", 2 * (i + 3))
                    covered(pool, "s_ps", 8 * (i + 1))
                    for g in range(NG):
                        G_.tensor_scalar(Hg[:, par, g, :].bitcast(F32R), HL[:, 0, :],
                                         C[:, C_GROUP + g:C_GROUP + g + 1], 0.0, op0=ALU.mult, op1=ALU.add)
                    W(pool, "lo_ready", i + 3)
                    if isinstance(i, int):
                        of_pair(pool, "qbd_in", i, par, 48)
                    G_.tensor_scalar(HLm[:, par, :, 0, :].bitcast(F32R), HL[:, 0:3, :], C[:, C_MASK:C_MASK + 1], 0.0,
                                     op0=ALU.mult, op1=ALU.add).then_inc(S["masked"], 1)
                    if early_norm(i):
                        bias()
                if on(i, 3) and not early_norm(i):
                    norm_factor()
                if on(i, -2) and not rows_last:
                    rows()
                if on(i, -1):
                    q = i - 1
                    covered(pool, "scattered", 32 * (i - 2))
                    for kk in range(2):
                        m = 2 * q + kk
                        srct = Tok[:, m:m + 1] if isinstance(m, int) else Tok[:, bass.ds(m, 1)]
                        ins = G_.tensor_copy(Row[:, b1, kk, 2 * D:ROW].bitcast(I32), srct)
                    ins.then_inc(S["numbered"], 1)
                    W(pool, "ln2_stats", i)
                    covered(pool, "x2n_ready", q)
                    G_.tensor_tensor(rstd2[:], mv2[:, :, 1], half, op=ALU.pow).then_inc(S["ln2_rstd"], 1)
                if on(i, -2) and rows_last:
                    rows()

            all_steps(pool, step)
            W(pool, "tables", 3)
            pool.wait_ge(S["w_in"], 16 * (2 * PAIRS + 1))

            def residual(m, c):
                e = pool.value_load(column(wexp_i, m, c), min_val=0, max_val=NE - 1)
                moved(pool, "g_in", m, c)
                if c >= NU:
                    W(pool, "y_ready", NG6 * m + c - NU + 1)
                G_.tensor_tensor(XB[:, c % NU, :], G[:, c % NG6, 0:D],
                                 B3[:, bass.ds(e, 1), :].rearrange("p a b -> p (a b)"),
                                 op=ALU.add).then_inc(S["xb_ready"], 1)

            def store(m, c):
                W(pool, "y_ready", NG6 * m + c + 1)
                G_.indirect_dma_start(
                    out=out,
                    out_offset=bass.IndirectOffsetOnAxis(ap=G[:, c % NG6, 2 * D:ROW].bitcast(I32), axis=0),
                    in_=OUT[:, c % NU, :], in_offset=None, bounds_check=TOKENS - 1, oob_is_err=False
                ).then_inc(S[f"stored{c % NG6}"], 16)

            def turn(m, c):
                if c >= NU:
                    store(m, c - NU)
                residual(m, c)
            all_tiles(pool, turn, NU, 0)
            for c in range(NT - NU, NT):
                store(0, c)
            for c in range(NT - NG6, NT):
                moved(pool, "stored", 0, c)


def kernel(**inputs):
    import numpy as np
    import concourse.bacc as bacc
    from concourse.bass_utils import run_bass_kernel_spmd

    a = {k: np.asarray(v) for k, v in inputs.items()}
    f = np.float32
    wq = a["L0_xattn_Wq"].reshape(NG, NJ, DH, D)
    wk = a["L0_xattn_Wk"].reshape(NG, NJ, DH, D)
    wv = a["L0_xattn_Wv"].reshape(8, 2, DH, D)
    wo = a["L0_xattn_Wo"].reshape(D, 8, 2, DH)
    bq = a["L0_xattn_bq"].reshape(NG, NJ, DH)
    bk = a["L0_xattn_bk"].reshape(NG, NJ, DH)
    bv = a["L0_xattn_bv"].reshape(8, 2, DH)
    rep = lambda v: np.broadcast_to(v.reshape(1, -1), (P, v.size))
    w1 = a["L0_ffn_W1"].transpose(1, 0, 2)
    w3 = a["L0_ffn_W3"].reshape(NE, 2, P, D).transpose(2, 0, 1, 3).reshape(P, NE, 2 * D)
    b1 = a["L0_ffn_b1"].reshape(NE, 4, P).transpose(2, 0, 1)
    b2 = a["L0_ffn_b2"].reshape(NE, 2, P).transpose(2, 0, 1)
    w2 = a["L0_ffn_W2"].reshape(NE, 4, P, D2).transpose(2, 0, 1, 3).reshape(P, NE, 4 * D2)
    p = np.arange(P)
    cst = np.zeros((P, C_ALL), f)
    cst[:, C_ID:C_ID + P] = np.eye(P)
    cst[:, C_LT:C_LT + P] = p[:, None] < p[None, :]
    cst[:, C_ONE:C_ONE + P] = 1
    cst[:, C_MASK:C_MASK + NJ] = ((p[:, None] >> 2) & 3) == np.arange(NJ)
    cst[:, C_GROUP:C_GROUP + NG] = (p[:, None] & 3) == np.arange(NG)
    cst[:, C_FIRST:C_FIRST + NE] = NE - np.arange(NE)
    cst[:, C_REGION:C_REGION + NE] = REGION * np.arange(NE)
    cst[:, C_TRI:C_TRI + 64] = (np.arange(NE)[None, :] <= np.arange(NE)[:, None]).reshape(1, 64)
    cst[:, C_JT:C_JT + NT] = np.arange(NT)
    cst[:, C_ROUND:C_ROUND + NE] = REGION * np.arange(NE) - (P - 1)
    cst[:, C_ROW:C_ROW + NT] = P * np.arange(NT)
    cst[:, C_HALF:C_HALF + 2] = -0.5
    arrays = {
        "x": a["x"].transpose(1, 0, 2),
        "ctxT": a["ctx_1024"].transpose(2, 0, 1).reshape(D, TOKENS),
        "wqT": wq.transpose(3, 2, 1, 0).reshape(D, D),
        "wkT": wk.transpose(3, 2, 1, 0).reshape(D, D),
        "wvT": wv.transpose(3, 0, 2, 1).reshape(D, D),
        "woT": wo.transpose(2, 1, 3, 0).reshape(D, D),
        "bqk": np.stack([bq.transpose(2, 1, 0).reshape(D), bk.transpose(2, 1, 0).reshape(D)], 1),
        "bv": rep(bv.transpose(0, 2, 1)),
        "bo": rep(a["L0_xattn_bo"]),
        "wr": a["L0_ffn_Wr"],
        "br": rep(a["L0_ffn_br"]),
        "wa": np.concatenate([w1, w3, b1, b2], 2),
        "w2": w2,
        "b3": np.broadcast_to(a["L0_ffn_b3"][None], (P, NE, D)),
        "cst": cst,
        "tok": (p[:, None] + P * np.arange(NB)[None, :]).astype(np.int32),
    }
    arrays = {k: np.ascontiguousarray(v) for k, v in arrays.items()}
    nc = bacc.Bacc("TRN2", target_bir_lowering=False, num_devices=1)
    aps = {k: nc.dram_tensor(f"in_{k}", v.shape, mybir.dt.from_np(v.dtype), kind="ExternalInput").ap()
           for k, v in arrays.items()}
    out = nc.dram_tensor("out", (TOKENS, D), F32, kind="ExternalOutput").ap()
    build(nc, out=out, **aps)
    r = run_bass_kernel_spmd(nc, [{f"in_{k}": v for k, v in arrays.items()}], core_ids=[0])
    return r.results[0]["out"].reshape(NB, P, D)
```
